# Optimizing a Trainium2 kernel written in Bass

```python
import numpy as np
import jax
import jax.numpy as jnp

def _softmax(x, axis=-1):
    return jax.nn.softmax(x, axis=axis)
def _gelu(x):
    return jax.nn.gelu(x, approximate=True)
def _silu(x):
    return jax.nn.silu(x)
def _sigmoid(x):
    return jax.nn.sigmoid(x)
def _layernorm(x, axis=-1, eps=1e-5):
    m = jnp.mean(x, axis=axis, keepdims=True)
    v = jnp.var(x, axis=axis, keepdims=True)
    return (x - m) / jnp.sqrt(v + eps)
def _scatter_add(tgt, idx, src, axis=0):
    return tgt.at[idx].add(src)
def _segment_sum(src, seg, n):
    return jax.ops.segment_sum(src, seg, n)

kernel_name = 'mk_adj_seq_d1_adj_512_ba5614'

def setup_inputs(seed: int = 0):
    np.random.seed(seed)
    _w = jnp.asarray
    def _rec_inputs():
        import jax
        import jax.numpy as jnp
        _gk = jax.random.key(seed)
        x = -0.0002928 + 1 * jax.random.normal(jax.random.fold_in(_gk, 1), (16, 1024, 512), jnp.float32)
        _w = (1.0 + jnp.arange(1024, dtype=jnp.float32)) ** -0.5
        _w = _w / _w.mean()
        _pij = jnp.clip(0.0078125 * _w[:, None] * _w[None, :], 0.0, 1.0)
        _a = jax.random.uniform(jax.random.fold_in(_gk, 2), (16, 1024, 1024)) < _pij
        _a = jnp.logical_or(_a, jnp.eye(1024, dtype=bool))
        adj = _a.astype(jnp.int32)
        return x, adj
    x, adj = _rec_inputs()
    def _L0_gnn_setup():
        import jax, jax.numpy as jnp
        import numpy as np
        B, N, D, H = (4, 2048, 512, 8)
        HD = D // H
        EPS = 1e-05
        key = jax.random.key(seed)
        ks = jax.random.split(key, 12)
        x = jax.random.normal(ks[0], (B, N, D), dtype=jnp.float32)
        adj = jax.random.randint(ks[1], (B, N, N), 0, 2, dtype=jnp.int32)
        adj = jnp.maximum(adj, jnp.eye(N, dtype=jnp.int32)[None, :, :])
        s = 1.0 / np.sqrt(D)
        Wq = jax.random.uniform(ks[2], (D, D), jnp.float32, -s, s)
        bq = jnp.zeros((D,), jnp.float32)
        Wk = jax.random.uniform(ks[3], (D, D), jnp.float32, -s, s)
        bk = jnp.zeros((D,), jnp.float32)
        Wv = jax.random.uniform(ks[4], (D, D), jnp.float32, -s, s)
        bv = jnp.zeros((D,), jnp.float32)
        Wo = jax.random.uniform(ks[5], (D, D), jnp.float32, -s, s)
        bo = jnp.zeros((D,), jnp.float32)
        gamma = jnp.ones((D,), jnp.float32)
        beta = jnp.zeros((D,), jnp.float32)
        return {'x': x, 'adj': adj, 'Wq': Wq, 'bq': bq, 'Wk': Wk, 'bk': bk, 'Wv': Wv, 'bv': bv, 'Wo': Wo, 'bo': bo, 'gamma': gamma, 'beta': beta}
    _L0_gnn_all = _L0_gnn_setup()
    _L0_gnn_in = {k: v for k, v in _L0_gnn_all.items() if k in ('Wq', 'bq', 'Wk', 'bk', 'Wv', 'bv', 'Wo', 'bo', 'gamma', 'beta', )}
    del _L0_gnn_all

    return {
        "x": x,
        "adj": adj,
        "L0_gnn_Wq": _L0_gnn_in["Wq"],
        "L0_gnn_bq": _L0_gnn_in["bq"],
        "L0_gnn_Wk": _L0_gnn_in["Wk"],
        "L0_gnn_bk": _L0_gnn_in["bk"],
        "L0_gnn_Wv": _L0_gnn_in["Wv"],
        "L0_gnn_bv": _L0_gnn_in["bv"],
        "L0_gnn_Wo": _L0_gnn_in["Wo"],
        "L0_gnn_bo": _L0_gnn_in["bo"],
        "L0_gnn_gamma": _L0_gnn_in["gamma"],
        "L0_gnn_beta": _L0_gnn_in["beta"],
    }

def reference(x, adj, L0_gnn_Wq, L0_gnn_bq, L0_gnn_Wk, L0_gnn_bk, L0_gnn_Wv, L0_gnn_bv, L0_gnn_Wo, L0_gnn_bo, L0_gnn_gamma, L0_gnn_beta):
    import jax
    import jax.numpy as jnp
    def _L0_gnn_ref(x, adj, Wq, bq, Wk, bk, Wv, bv, Wo, bo, gamma, beta):
        import jax, jax.numpy as jnp
        import numpy as np
        B, N, D, H = (4, 2048, 512, 8)
        HD = D // H
        EPS = 1e-05
        b, n, d = x.shape
        scale = 1.0 / np.sqrt(HD).astype(np.float32)
        q = (x @ Wq + bq).reshape(b, n, H, HD)
        k = (x @ Wk + bk).reshape(b, n, H, HD)
        v = (x @ Wv + bv).reshape(b, n, H, HD)
        scores = jnp.einsum('bnhd,bmhd->bhnm', q, k) * scale
        mask = (adj == 0)[:, None, :, :]
        scores = jnp.where(mask, jnp.float32(-jnp.inf), scores)
        attn = jax.nn.softmax(scores, axis=-1)
        h = jnp.einsum('bhnm,bmhd->bnhd', attn, v).reshape(b, n, d)
        h = h @ Wo + bo
        y = h + x
        mu = jnp.mean(y, axis=-1, keepdims=True)
        var = jnp.mean(jnp.square(y - mu), axis=-1, keepdims=True)
        return (y - mu) * jax.lax.rsqrt(var + EPS) * gamma + beta

    x = _L0_gnn_ref(x, adj, L0_gnn_Wq, L0_gnn_bq, L0_gnn_Wk, L0_gnn_bk, L0_gnn_Wv, L0_gnn_bv, L0_gnn_Wo, L0_gnn_bo, L0_gnn_gamma, L0_gnn_beta)
    return x


_drawn_inputs = setup_inputs


def setup_inputs(seed=0):
    import zlib

    import numpy as np

    out = dict(_drawn_inputs(seed))
    spreads = {'L0_gnn_bq': (0.0, 0.8),
     'L0_gnn_bk': (0.0, 0.8),
     'L0_gnn_bv': (0.0, 0.1),
     'L0_gnn_bo': (0.0, 0.1),
     'L0_gnn_gamma': (1.0, 0.2),
     'L0_gnn_beta': (0.0, 0.1)}
    factors = {}
    for name, (base, spread) in spreads.items():
        noise = np.random.default_rng([zlib.crc32(name.encode()), seed]).standard_normal(out[name].shape)
        drawn = base * np.exp(spread * noise) if base else spread * noise
        out[name] = jnp.asarray(drawn.astype(out[name].dtype))
    for name, factor in factors.items():
        out[name] = (out[name] * factor).astype(out[name].dtype)
    return out
```

```python
from contextlib import ExitStack

import concourse.bass as bass
from concourse import mybir

F32 = mybir.dt.float32
F16 = mybir.dt.float16
BF16 = mybir.dt.bfloat16
I32 = mybir.dt.int32
U8 = mybir.dt.uint8
ALU = mybir.AluOpType
ACT = mybir.ActivationFunctionType
AX = mybir.AxisListType
ABSMAX = bass.bass_isa.ReduceOp.absmax

P = 128
HALF = 512
MASKED = -(2.0 ** 100)
SHIFT_UNIT = 2.0 ** 15
LN64 = 4.1588830833596715
EPS = 1e-5


class Sem:

    def __init__(self, handle, per, credit=0):
        self.h, self.per, self.credit = handle, per, credit

    def at(self, b, k):
        return b * self.per + (self.credit + k)


def gnn_attention(nc, x, adj, Wq, bq, Wk, bk, Wv, bv, Wo, bo, gamma, beta, out):
    B, N, D = x.shape
    H = 8
    HD = D // H
    NT = N // P
    KT = D // P
    PAIRS = H // 2
    CHUNKS = H * 2 * (NT // 2)
    VW = 2 * HD + 2
    OW = HD + 1
    XR = 3
    XT = 3 * NT
    assert HD == 64 and NT == 8 and KT == 4 and XT % XR == 0

    ctx = ExitStack()
    with ctx:
        def sb(name, shape, dt):
            return ctx.enter_context(nc.sbuf_tensor(name, shape, dt))

        def ps(name, shape, dt):
            return ctx.enter_context(nc.psum_tensor(name, shape, dt))

        def sem(name, per=0, credit=0):
            return Sem(ctx.enter_context(nc.semaphore(name)), per, credit)

        w_hi = sb("w_hi", [P, 4, KT, D], F16)
        w_lo = sb("w_lo", [P, 4, KT, D], F16)
        xt_hi = sb("xt_hi", [P, KT, N], F16)
        xt_lo = sb("xt_lo", [P, KT, N], F16)
        q1 = [sb(f"q1_{i}", [P, N], F16) for i in range(4)]
        q2 = [sb(f"q2_{i}", [P, N], F16) for i in range(4)]
        k1 = [sb(f"k1_{i}", [P, N], F16) for i in range(4)]
        k2 = [sb(f"k2_{i}", [P, N], F16) for i in range(4)]
        stage = sb("stage", [P, 2, 2, N], F16)
        proj = sb("proj", [P, 2, HALF], F32)
        vt = sb("vt", [P, NT, H, VW], F16)
        mask_n = sb("mask_n", [P, NT, N], BF16)
        mask_t = sb("mask_t", [P, NT, N], U8)
        ex = sb("ex", [P, 2, N], F32)
        pr_hi = [sb(f"pr_hi{i}", [P, NT, HALF], F16) for i in range(2)]
        pr_lo = [sb(f"pr_lo{i}", [P, NT, HALF], F16) for i in range(2)]
        att = sb("att", [P, NT, D], F32)
        xr = sb("xr", [P, XR, D], F32)
        ar = sb("ar", [P, 2, HALF], I32)
        gamma_b = sb("gamma_b", [P, D], F32)
        beta_b = sb("beta_b", [P, D], F32)
        bo_b = sb("bo_b", [P, D], F32)
        id32 = sb("id32", [P, P], F32)
        id16 = sb("id16", [P, P], F16)
        idbf = sb("idbf", [P, P], BF16)
        b_t = sb("b_t", [P, 3, KT], F32)
        beta_t = sb("beta_t", [P, 2, KT], F32)
        amax = sb("amax", [P, 8], F32)
        xmax = sb("xmax", [P, NT], F32)
        gmax = sb("gmax", [P, 8], F32)
        sw = sb("sw", [P, 4], F32)
        rw = sb("rw", [P, 4], F32)
        c4 = sb("c4", [P, 4], F32)
        d4 = sb("d4", [P, 4], F32)
        target4 = sb("target4", [P, 4], F32)
        cap4 = sb("cap4", [P, 4], F32)
        bound = sb("bound", [P, 4], F32)
        expo = sb("expo", [P, 4], I32)
        sc = sb("sc", [P, 4], F32)
        rx = sb("rx", [P, 1], F32)
        alpha = sb("alpha", [P, 3], F32)
        sqk = sb("sqk", [P, 1], F32)
        gsc = sb("gsc", [P, 1], F32)
        so = sb("so", [P, 1], F32)
        ao = sb("ao", [P, 1], F32)
        ones8 = sb("ones8", [P, NT], F32)
        gam = sb("gam", [P, NT], F32)
        shl = sb("shl", [P, NT, 32], F16)
        rinv = sb("rinv", [P, NT // 2], F32)
        stats = sb("stats", [P, 2, 6], F32)
        mv = sb("mv", [P, 2, 2], F32)
        vpe = sb("vpe", [P, 2], F32)
        rstd = sb("rstd", [P, 2], F32)
        mhalf = sb("mhalf", [P, 1], F32)
        eps = sb("eps", [P, 1], F32)
        yr = ex[:, :, :].rearrange("p a (c n) -> p (a c) n", n=D)
        ot_hi, ot_lo = [[stage[:, i // 2, part, i % 2 * D:(i % 2 + 1) * D].rearrange("p (k n) -> p k n", n=P)
                         for i in range(4)] for part in range(2)]
        w32 = [t[:, :, :].rearrange("p a n -> p (a n)").bitcast(F32)
               for t in (pr_hi[0], pr_hi[1], pr_lo[0], pr_lo[1])]
        bv_rep = att[:, 0, :].rearrange("p (k n) -> p k n", n=P)

        st = [ps(f"st{i}", [P, 2, HALF], F32) for i in range(2)]
        mx = ps("mx", [P, 2, HALF], F32)
        op = ps("op", [P, HALF], F32)
        gp = ps("gp", [P, HALF], F32)
        st_bank = [st[i // 2][:, i % 2, :] for i in range(4)]
        og_bank = [op[:, :], gp[:, :]]
        gp_bf = gp[:, :].bitcast(BF16).rearrange("p (t n) -> p t n", n=P)
        st_bf = [t.bitcast(BF16).rearrange("p (t n) -> p t n", n=P) for t in st_bank]

        w_in = [sem(f"w_in{i}") for i in range(4)]
        small_in = sem("small_in")
        x_in = [sem(f"x_in{i}", 16 * XT // XR, 16 * ((2 * NT - 1 - i) // XR + 1)) for i in range(XR)]
        a_in = [sem(f"a_in{i}", 16 * NT, 16 * NT) for i in range(2)]
        k_in = [sem(f"k_in{i}", 2 * 48) for i in range(4)]
        q_in = [sem(f"q_in{i}", 2 * 48) for i in range(4)]
        y_out = [sem(f"y_out{i}", 2 * 16, 16) for i in range(4)]
        zeroed = sem("zeroed")
        consts = sem("consts")
        dconst = sem("dconst")
        amaxed = sem("amaxed")
        gmaxed = sem("gmaxed", 1, 1)
        whi = sem("whi")
        wlo = sem("wlo")
        bvrep = sem("bvrep")
        bvwo = sem("bvwo")
        bo_ready = sem("bo_ready")
        scaled = sem("scaled", 1, 1)
        rescaled = sem("rescaled", 1)
        dl = sem("dl")
        dve_wait = sem("dve_wait")
        pool_wait = sem("pool_wait")
        sp_wait = sem("sp_wait")
        dlb = sem("dlb", 7, 6)
        masked_n = sem("masked_n", 2 * NT, 2 * NT + 2)
        xt_ps = sem("xt_ps", NT, NT)
        xt_h = sem("xt_h", NT, NT)
        xt_l = sem("xt_l", NT, NT)
        mt_ps = sem("mt_ps", NT, NT)
        mt_sb = sem("mt_sb", NT, NT)
        grp = sem("grp", 4 * PAIRS)
        grp32 = sem("grp32", 4 * PAIRS)
        grp_h = sem("grp_h", 4 * PAIRS)
        grp_l = sem("grp_l", 4 * PAIRS, 2)
        v_ps = sem("v_ps", NT)
        v_h = sem("v_h", NT)
        v_l = sem("v_l", NT)
        mx_ps = sem("mx_ps", CHUNKS)
        mx_done = sem("mx_done", CHUNKS)
        gam_h = sem("gam_h", 2 * H)
        gam_l = sem("gam_l", 2 * H)
        sh_ps = sem("sh_ps", 2 * H, 2)
        sh_sb = sem("sh_sb", 2 * H)
        st_ps = sem("st_ps", CHUNKS)
        st_mk = sem("st_mk", CHUNKS)
        ex_sb = sem("ex_sb", CHUNKS, 1)
        p_h = sem("p_h", CHUNKS, 2)
        p_l = sem("p_l", CHUNKS, 2)
        pv = sem("pv", 4 * H, 4)
        o_inv = sem("o_inv", 2 * H)
        o_sb = sem("o_sb", 2 * H, 1)
        xmaxed = sem("xmaxed", NT)
        xm_all = sem("xm_all", 1)
        ot_ps = sem("ot_ps", NT)
        ot_h = sem("ot_h", NT, 1)
        ot_l = sem("ot_l", NT, 1)
        z_ps = sem("z_ps", NT)
        xb = sem("xb", NT)
        y_sb = sem("y_sb", NT, 4)
        y_st = sem("y_st", NT)
        y_mv = sem("y_mv", NT)
        y_ve = sem("y_ve", NT)
        y_rs = sem("y_rs", NT)
        y_ga = sem("y_ga", NT)
        y_be = sem("y_be", NT)

        GROUPS = [(w, f) for w in (1, 0) for f in range(2)]

        def slot(h):
            return h % 4

        def own(h):
            a = HD * (h % 2)
            return slice(a, a + HD), slice(HD - a, 2 * HD - a)

        def shift_rows(h):
            a = HD * (1 - h % 2)
            return slice(a, a + 32)

        STEPS = [(h, s) for h in range(H) for s in range(8)]

        def max_tile(h, s):
            return 2 * h + s // 4 if h < 4 and s % 4 == 2 else None

        def mt_bank(t):
            return gp_bf if t < 4 else st_bf[t - 4]

        def group_of(h, s):
            u = 2 * h + s // 4
            return 7 + u if 1 <= u <= 8 else None

        def in_batch(b):
            return not (isinstance(b, int) and b == -1)

        block = ctx.enter_context(nc.Block())

        @block.sync
        def _(sp):
            for i, w in enumerate((Wq, Wk, Wv, Wo)):
                sp.dma_start(w32[i].rearrange("p (k n) -> p k n", n=D),
                             w.rearrange("(k p) n -> p k n", p=P)).then_inc(w_in[i].h, 16)
            with nc.allow_non_contiguous_dma(reason="biases by feature, once"):
                for i, v in enumerate((bq, bk, bv)):
                    sp.dma_start(b_t[:, i, :], v.rearrange("(k p) -> p k", p=P)).then_inc(small_in.h, 16)
            for t, v in ((gamma_b, gamma), (beta_b, beta), (bo_b, bo)):
                sp.dma_start(t[:, :], v.partition_broadcast(P)).then_inc(small_in.h, 16)
            for n in range(2 * NT):
                t = n % NT
                if XR <= n < NT + XR:
                    sp.wait_ge(amaxed.h, n - XR + 1)
                if n >= NT + XR:
                    sp.wait_ge(xt_ps.h, xt_ps.at(-1, t - XR + 1))
                sp.dma_start(xr[:, n % XR, :], x[0, t * P:(t + 1) * P, :]).then_inc(x_in[n % XR].h, 16)
                if n >= NT:
                    for f in range(2):
                        if t:
                            sp.wait_ge(masked_n.h, masked_n.at(-1, 2 * t + f - 1))
                        sp.dma_start(ar[:, f, :], adj[0, t * P:(t + 1) * P, f * HALF:(f + 1) * HALF])\
                            .then_inc(a_in[f].h, 16)
            sp.wait_ge(xt_ps.h, xt_ps.at(-1, NT))

            with sp.Fori(0, B) as b:
                def load_x(n, batch, t):
                    sp.dma_start(xr[:, n % XR, :], x[batch, t * P:(t + 1) * P, :]).then_inc(x_in[n % XR].h, 16)

                def arrange(h, which):
                    src, far = own(h)
                    hi, lo = stage[src, which, 0, :], stage[src, which, 1, :]
                    if which == 0:
                        places, done = ((k1[slot(h)][src, :], hi), (k1[slot(h)][far, :], hi),
                                        (k2[slot(h)][src, :], lo)), k_in[slot(h)]
                    else:
                        places, done = ((q1[slot(h)][src, :], hi), (q1[slot(h)][far, :], lo),
                                        (q2[slot(h)][src, :], hi)), q_in[slot(h)]
                    for dst, part in places:
                        sp.dma_start(dst, part).then_inc(done.h, 16)

                nxt = (b + 1) % B

                def max_load(t):
                    if t < XR:
                        sp.wait_ge(y_sb.h, y_sb.at(b, t - XR + 1))
                    else:
                        sp.wait_ge(xmaxed.h, xmaxed.at(b, t - XR + 1))
                    load_x(t, nxt, t)

                def transpose_load(t):
                    if t < XR:
                        sp.wait_ge(xmaxed.h, xmaxed.at(b, NT - XR + t + 1))
                    else:
                        sp.wait_ge(xt_ps.h, xt_ps.at(b, t - XR + 1))
                    load_x(NT + t, nxt, t)

                def adjacency_load(t):
                    for f in range(2):
                        sp.wait_ge(masked_n.h, masked_n.at(b, 2 * t + f - 1))
                        sp.dma_start(ar[:, f, :], adj[nxt, t * P:(t + 1) * P, f * HALF:(f + 1) * HALF])\
                            .then_inc(a_in[f].h, 16)

                for j in range(2):
                    for which in range(2):
                        sp.wait_ge(grp_l.h, grp_l.at(b, 4 * j + 2 * which + 2))
                        for h in (2 * j, 2 * j + 1):
                            arrange(h, which)
                for t in range(7):
                    max_load(t)
                sp.wait_ge(grp_l.h, grp_l.at(b, 10))
                sp.sem_inc(sp_wait.h, 1)
                sp.wait_ge(st_ps.h, st_ps.at(b, 8))
                arrange(4, 0)
                max_load(7)
                sp.wait_ge(grp_l.h, grp_l.at(b, 12))
                arrange(4, 1)
                sp.wait_ge(st_ps.h, st_ps.at(b, 16))
                arrange(5, 0)
                arrange(5, 1)
                for t in range(XR):
                    transpose_load(t)
                adjacency_load(0)
                sp.wait_ge(grp_l.h, grp_l.at(b, 14))
                sp.sem_inc(sp_wait.h, 1)
                sp.wait_ge(st_ps.h, st_ps.at(b, 24))
                arrange(6, 0)
                sp.wait_ge(grp_l.h, grp_l.at(b, 16))
                arrange(6, 1)
                sp.wait_ge(st_ps.h, st_ps.at(b, 32))
                arrange(7, 0)
                arrange(7, 1)
                for t in range(1, NT):
                    if t + XR - 1 < NT:
                        transpose_load(t + XR - 1)
                    adjacency_load(t)
                for t in range(NT):
                    if t < XR:
                        sp.wait_ge(xt_ps.h, xt_ps.at(b, NT - XR + t + 1))
                    else:
                        sp.wait_ge(y_sb.h, y_sb.at(b, t - XR + 1))
                    load_x(2 * NT + t, b, t)
            for i in range(4):
                sp.wait_ge(y_out[i].h, y_out[i].at(B, 0))

        @block.tensor
        def _(pe):
            mm = nc.tensor.matmul
            pe.wait_ge(bvrep.h, 1)
            pe.wait_ge(w_in[3].h, 16)
            for k in range(KT):
                last = mm(op[:, :], bv_rep[:, k, :], w32[3][:, k * D:(k + 1) * D], start=(k == 0), stop=(k == KT - 1))
            last.then_inc(bvwo.h, 1)
            pe.wait_ge(consts.h, 3)
            pe.wait_ge(whi.h, 4)
            pe.wait_ge(wlo.h, 4)
            pe.wait_ge(bo_ready.h, 1)
            pe.sem_inc(sh_ps.h, sh_ps.credit)

            def x_transpose(b, t, loads_before):
                n = NT + t
                pe.wait_ge(x_in[n % XR].h, loads_before + 16 * (n // XR + 1))
                if t >= 2:
                    pe.wait_ge(xt_h.h, xt_h.at(b, t - 1))
                    pe.wait_ge(xt_l.h, xt_l.at(b, t - 1))
                for k in range(KT):
                    last = mm(mx[:, t % 2, k * P:(k + 1) * P], xr[:, n % XR, k * P:(k + 1) * P],
                              id32[:, :], is_transpose=True, start=True, stop=True)
                last.then_inc(xt_ps.h, 1)

            def mask_transpose(b, t):
                pe.wait_ge(masked_n.h, masked_n.at(b, 2 * t + 2))
                if 1 <= t < 4:
                    pe.wait_ge(mt_sb.h, mt_sb.at(b, t))
                elif t >= 4 and in_batch(b):
                    pe.wait_ge(ex_sb.h, ex_sb.at(b, CHUNKS - 1 + (t - 4) // 2))
                for m in range(NT):
                    last = mm(mt_bank(t)[:, m, :], mask_n[:, t, m * P:(m + 1) * P], idbf[:, :],
                              is_transpose=True, start=True, stop=True)
                last.then_inc(mt_ps.h, 1)

            for t in range(NT):
                x_transpose(-1, t, 0)
            for t in range(NT):
                mask_transpose(-1, t)

            with pe.Fori(0, B) as b:
                def group(g, bank, parts):
                    w, f = GROUPS[g % 4]
                    cols = slice((g // 4) * P, (g // 4 + 1) * P)
                    steps = [(a, c, k) for a, c in ((w_hi, xt_hi), (w_hi, xt_lo), (w_lo, xt_hi)) for k in range(KT)]
                    for n in parts:
                        a, c, k = steps[n]
                        last = mm(bank, a[:, w, k, cols], c[:, k, f * HALF:(f + 1) * HALF],
                                  start=(n == 0), stop=(n == 3 * KT - 1))
                    if parts[-1] == 3 * KT - 1:
                        last.then_inc(grp.h, 1)

                def v_tile(t):
                    if t < 2:
                        pe.wait_ge(o_sb.h, o_sb.at(b, 0))
                    else:
                        pe.wait_ge(v_l.h, v_l.at(b, t - 1))
                    if t == 6:
                        pe.wait_ge(sh_sb.h, sh_sb.at(b, 1))
                    n = 0
                    for a, c in ((xt_hi, w_hi), (xt_hi, w_lo), (xt_lo, w_hi)):
                        for k in range(KT):
                            last = mm(og_bank[t % 2], a[:, k, t * P:(t + 1) * P], c[:, 2, k, :],
                                      start=(n == 0), stop=(n == 3 * KT - 1))
                            n += 1
                    last.then_inc(v_ps.h, 1)

                def maxima(h, t):
                    if t == 0:
                        pe.wait_ge(k_in[slot(h)].h, k_in[slot(h)].at(b, 48 * (h // 4 + 1)))
                        pe.wait_ge(q_in[slot(h)].h, q_in[slot(h)].at(b, 48 * (h // 4 + 1)))
                    if h == 0 and t == 0:
                        pe.wait_ge(ot_l.h, ot_l.at(b, 0))
                        pe.wait_ge(ot_h.h, ot_h.at(b, 0))
                    else:
                        pe.wait_ge(mx_done.h, mx_done.at(b, 8 * h + t))
                    for f in range(2):
                        last = mm(mx[:, f, :], q1[slot(h)][:, t * P:(t + 1) * P],
                                  k1[slot(h)][:, f * HALF:(f + 1) * HALF], start=True, stop=True)
                    last.then_inc(mx_ps.h, 1)

                def shift(h, f):
                    pe.wait_ge(gam_l.h, gam_l.at(b, 2 * h + f + 1))
                    if h == 0 and f == 0:
                        pe.wait_ge(v_l.h, v_l.at(b, 5))
                    elif h == 0:
                        pe.wait_ge(v_l.h, v_l.at(b, NT))
                    elif (h, f) == (1, 0):
                        pe.wait_ge(sh_sb.h, sh_sb.at(b, 2))
                    else:
                        pe.wait_ge(o_sb.h, o_sb.at(b, 2 * h + f - 2))
                    for t in range(4):
                        last = mm(op[shift_rows(h), t * P:(t + 1) * P], shl[:, 4 * f + t, :], id16[:, :],
                                  start=True, stop=True)
                    last.then_inc(sh_ps.h, 1)

                def chunk(h, s):
                    c = 8 * h + s
                    f, i = s // 4, s % 4
                    if c < 2:
                        pe.wait_ge(grp32.h, grp32.at(b, 6 + 2 * c))
                    else:
                        pe.wait_ge(ex_sb.h, ex_sb.at(b, c - 1))
                    if i == 0:
                        pe.wait_ge(sh_sb.h, sh_sb.at(b, 2 * h + f + 1))
                    n = slice(f * HALF, (f + 1) * HALF)
                    for a in range(2):
                        m = slice((2 * i + a) * P, (2 * i + a + 1) * P)
                        mm(st[c % 2][:, a, :], k1[slot(h)][:, m], q1[slot(h)][:, n], start=True, stop=False)
                        last = mm(st[c % 2][:, a, :], k2[slot(h)][:, m], q2[slot(h)][:, n], start=False, stop=True)
                    last.then_inc(st_ps.h, 1)

                def values(u, part):
                    h = u // 2
                    if part == 0:
                        pe.wait_ge(p_h.h, p_h.at(b, 4 * u + 4))
                        pe.wait_ge(p_l.h, p_l.at(b, 4 * u + 4))
                        pe.wait_ge(sh_sb.h, sh_sb.at(b, min(u + 3, 2 * H)))
                        pe.wait_ge(o_sb.h, o_sb.at(b, u))
                    for t in (2 * part, 2 * part + 1):
                        n = slice(t * P, (t + 1) * P)
                        o = op[:, t * OW:(t + 1) * OW]
                        for m in range(NT):
                            mm(o, pr_hi[u % 2][:, m, n], vt[:, m, h, HD:2 * HD + 1], start=(m == 0), stop=False)
                            mm(o[:, 0:HD], pr_hi[u % 2][:, m, n], vt[:, m, h, 0:HD], start=False, stop=False)
                            last = mm(o, pr_lo[u % 2][:, m, n], vt[:, m, h, HD:2 * HD + 1],
                                      start=False, stop=(m == NT - 1))
                    last.then_inc(pv.h, 1)

                pe.wait_ge(xt_h.h, xt_h.at(b, 0))
                pe.wait_ge(xt_l.h, xt_l.at(b, 0))
                pe.wait_ge(mt_sb.h, mt_sb.at(b, 0))
                for g in range(4):
                    pe.wait_ge(y_sb.h, y_sb.at(b, g - 3))
                    group(g, st_bank[g], range(12))
                for t in range(4):
                    v_tile(t)
                for t in range(4):
                    pe.wait_ge(grp32.h, grp32.at(b, t + 1))
                    group(4 + t, st_bank[t], range(12))
                    maxima(0, t)
                for t in range(4, NT):
                    if t == 6:
                        shift(0, 0)
                    v_tile(t)
                    maxima(0, t)
                for h, s in STEPS:
                    u = 2 * h + s // 4
                    chunk(h, s)
                    if h < H - 1:
                        maxima(h + 1, s)
                    if s == 1:
                        shift(h, 1)
                    if s == 5 and h < H - 1:
                        shift(h + 1, 0)
                    g = group_of(h, s)
                    if g is not None and s % 4 < 2:
                        if s % 4 == 0:
                            if g == 8:
                                pe.wait_ge(v_l.h, v_l.at(b, NT))
                            else:
                                pe.wait_ge(grp32.h, grp32.at(b, g))
                        group(g, gp[:, :], range(6 * (s % 4), 6 * (s % 4) + 6))
                    if h == H - 1:
                        if s == 0:
                            pe.wait_ge(mx_done.h, mx_done.at(b, CHUNKS))
                        x_transpose(b, s, x_in[(NT + s) % XR].at(b, 0))
                        if s == 4:
                            pe.wait_ge(grp32.h, grp32.at(b, 4 * PAIRS))
                        if s >= 4:
                            mask_transpose(b, s - 4)
                    if s % 4 >= 2 and u >= 1:
                        values(u - 1, s % 4 - 2)
                def att_transpose(t):
                    if t < 2:
                        pe.wait_ge(xt_h.h, xt_h.at(b, 7 + t))
                        pe.wait_ge(xt_l.h, xt_l.at(b, 7 + t))
                    else:
                        pe.wait_ge(ot_h.h, ot_h.at(b, t - 1))
                        pe.wait_ge(ot_l.h, ot_l.at(b, t - 1))
                    pe.wait_ge(o_sb.h, o_sb.at(b, 2 * H - 1 + t // 4))
                    for k in range(KT):
                        last = mm(mx[:, t % 2, k * P:(k + 1) * P], att[:, t, k * P:(k + 1) * P],
                                  id32[:, :], is_transpose=True, start=True, stop=True)
                    last.then_inc(ot_ps.h, 1)

                def output(z):
                    if z < 4:
                        pe.wait_ge(mt_sb.h, mt_sb.at(b, 4 + z + 1))
                    else:
                        pe.wait_ge(y_sb.h, y_sb.at(b, z - 3))
                    pe.wait_ge(ot_h.h, ot_h.at(b, z + 1))
                    pe.wait_ge(ot_l.h, ot_l.at(b, z + 1))
                    n = 0
                    for a, c in ((ot_hi, w_hi), (ot_hi, w_lo), (ot_lo, w_hi)):
                        for k in range(KT):
                            last = mm(st_bank[z % 4], a[z % 4][:, k, :], c[:, 3, k, :],
                                      start=(n == 0), stop=(n == 3 * KT - 1))
                            n += 1
                    last.then_inc(z_ps.h, 1)

                att_transpose(0)
                att_transpose(1)
                for t in range(4, NT):
                    mask_transpose(b, t)
                for part in range(2):
                    values(2 * H - 1, part)
                for t in range(NT):
                    output(t)
                    if t + 2 < NT:
                        att_transpose(t + 2)

        @block.scalar
        def _(act):
            a = nc.scalar.activation
            act.wait_ge(dconst.h, 1)
            for i in range(4):
                a(w_hi[:, i, :, :].rearrange("p k n -> p (k n)"), w32[i], ACT.Copy, scale=sw[:, i:i + 1])\
                    .then_inc(whi.h, 1)
            act.sem_inc(ex_sb.h, ex_sb.credit)
            act.sem_inc(p_h.h, p_h.credit)
            act.sem_inc(ot_h.h, ot_h.credit)
            for i in range(4):
                act.sem_inc(y_out[i].h, y_out[i].credit)

            def x_hi(b, t):
                if t == 0:
                    act.wait_ge(scaled.h, scaled.at(b, 1))
                act.wait_ge(xt_ps.h, xt_ps.at(b, t + 1))
                a(xt_hi[:, :, t * P:(t + 1) * P], mx[:, t % 2, :].rearrange("p (k n) -> p k n", n=P),
                  ACT.Copy, scale=sc[:, 0:1]).then_inc(xt_h.h, 1)

            def mask_out(b, t):
                act.wait_ge(mt_ps.h, mt_ps.at(b, t + 1))
                a(mask_t[:, :, t * P:(t + 1) * P], mt_bank(t), ACT.Copy, scale=1.0 / MASKED)\
                    .then_inc(mt_sb.h, 1)

            for t in range(NT):
                x_hi(-1, t)
            for t in range(NT):
                mask_out(-1, t)

            with act.Fori(0, B) as b:
                def group32(g):
                    w, _ = GROUPS[g % 4]
                    act.wait_ge(grp.h, grp.at(b, g + 1))
                    act.wait_ge(grp_l.h, grp_l.at(b, g - 1))
                    bank = st_bank[g % 4] if g < 8 else gp[:, :]
                    a(proj[:, g % 2, :], bank, ACT.Identity, bias=beta_t[:, w, g // 4:g // 4 + 1],
                      scale=alpha[:, w:w + 1]).then_inc(grp32.h, 1)

                def group_hi(g):
                    w, f = GROUPS[g % 4]
                    which = 1 - w
                    act.wait_ge(grp32.h, grp32.at(b, g + 1))
                    if g >= 4:
                        h = 2 * (g // 4 - 1)
                        done = (k_in, q_in)[which]
                        for hh in (h, h + 1):
                            act.wait_ge(done[slot(hh)].h, done[slot(hh)].at(b, 48 * (hh // 4 + 1)))
                    a(stage[:, which, 0, f * HALF:(f + 1) * HALF], proj[:, g % 2, :], ACT.Copy).then_inc(grp_h.h, 1)

                def shift_hi(h, f):
                    act.wait_ge(mx_done.h, mx_done.at(b, 8 * h + 4 * f + 4))
                    act.wait_ge(sh_ps.h, sh_ps.at(b, 2 * h + f - 1))
                    a(shl[:, 4 * f:4 * f + 4, 0], gam[:, 4 * f:4 * f + 4], ACT.Copy).then_inc(gam_h.h, 1)

                def shift_out(h, f):
                    act.wait_ge(sh_ps.h, sh_ps.at(b, 2 * h + f + 1))
                    a(q2[slot(h)][shift_rows(h), f * HALF:(f + 1) * HALF], op[shift_rows(h), :], ACT.Copy)\
                        .then_inc(sh_sb.h, 1)

                def v_hi(t):
                    act.wait_ge(v_ps.h, v_ps.at(b, t + 1))
                    a(vt[:, t, :, HD:2 * HD], og_bank[t % 2].rearrange("p (h d) -> p h d", d=HD), ACT.Copy,
                      scale=alpha[:, 2:3]).then_inc(v_h.h, 1)

                group32(0)
                for g in range(1, 4):
                    group32(g)
                    group_hi(g - 1)
                group_hi(3)
                for t in range(4):
                    v_hi(t)
                group32(4)
                for g in range(5, 8):
                    group32(g)
                    group_hi(g - 1)
                group_hi(7)
                shift_hi(0, 0)
                v_hi(4)
                v_hi(5)
                shift_out(0, 0)
                v_hi(6)
                v_hi(7)
                for h, s in STEPS:
                    c, u = 8 * h + s, 2 * h + s // 4
                    if s == 0:
                        shift_hi(h, 1)
                    if s == 4 and h < H - 1:
                        shift_hi(h + 1, 0)
                    if s == 1:
                        shift_out(h, 1)
                    if s == 5 and h < H - 1:
                        shift_out(h + 1, 0)
                    act.wait_ge(st_mk.h, st_mk.at(b, c + 1))
                    act.wait_ge(p_l.h, p_l.at(b, c - 1))
                    act.wait_ge(p_h.h, p_h.at(b, c - 1))
                    if c == 0:
                        act.wait_ge(rescaled.h, rescaled.at(b, 1))
                    if c < 2:
                        for i in (2 * c, 2 * c + 1):
                            act.wait_ge(y_out[i].h, y_out[i].at(b, 0))
                    a(ex[:, c % 2, :], st[c % 2][:, :, :].rearrange("p a n -> p (a n)"), ACT.Exp,
                      scale=gsc[:, 0:1]).then_inc(ex_sb.h, 1)
                    act.wait_ge(ex_sb.h, ex_sb.at(b, c + 1))
                    act.wait_ge(pv.h, pv.at(b, 2 * (u - 1)))
                    a(pr_hi[u % 2][:, 2 * (s % 4):2 * (s % 4) + 2, :].rearrange("p a n -> p (a n)"),
                      ex[:, c % 2, :], ACT.Copy).then_inc(p_h.h, 1)
                    g = group_of(h, s)
                    if g is not None and s % 4 == 2:
                        group32(g)
                    if g is not None and s % 4 == 3:
                        group_hi(g)
                    if h == H - 1:
                        x_hi(b, s)
                        if s >= 4:
                            mask_out(b, s - 4)
                def att_hi(t):
                    act.wait_ge(ot_ps.h, ot_ps.at(b, t + 1))
                    if t >= 4:
                        act.wait_ge(z_ps.h, z_ps.at(b, t - 3))
                    a(ot_hi[t % 4], mx[:, t % 2, :].rearrange("p (k n) -> p k n", n=P), ACT.Copy)\
                        .then_inc(ot_h.h, 1)

                def write_rows(t):
                    act.wait_ge(y_be.h, y_be.at(b, t + 1))
                    act.dma_start(out[b, t * P:(t + 1) * P, :], yr[:, t % 4, :]).then_inc(y_out[t % 4].h, 16)

                att_hi(0)
                att_hi(1)
                for t in range(4, NT):
                    mask_out(b, t)
                for t in range(2, NT):
                    att_hi(t)
                    if t >= 5:
                        write_rows(t - 5)
                for t in range(NT - 5, NT):
                    write_rows(t)

        @block.vector
        def _(dve):
            v = nc.vector
            chain = [0]

            def link(ins):
                chain[0] += 1
                ins.then_inc(dl.h, 1)
                dve.wait_ge(dl.h, chain[0])

            v.memset(vt[:, :, :, :].rearrange("p t h w -> p (t h w)"), 1.0)
            v.memset(shl[:, :, :].rearrange("p t n -> p (t n)"), 0.0)
            v.memset(ones8[:, :], 1.0)
            v.memset(mhalf[:, :], -0.5)
            v.memset(eps[:, :], EPS)
            v.memset(amax[:, :], 0.0)
            v.memset(target4[:, :], 268.0)
            v.memset(cap4[:, :], 167.0)
            v.memset(d4[:, :], 0.0)
            v.memset(c4[:, :], 1.0)
            for i in range(4):
                a = HD * (1 - i % 2)
                v.memset(k2[i][a:a + HD, :], 0.0)
                v.memset(q2[i][a:a + HD, :], 0.0)
            link(v.memset(xmax[:, :], 0.0))
            v.memset(target4[:, 1:3], 265.0)
            v.memset(cap4[:, 1:3], 139.0)
            for i in range(4):
                a = HD * (1 - i % 2)
                v.memset(k2[i][a:a + 3, :], SHIFT_UNIT)

            for t in range(NT):
                dve.wait_ge(x_in[t % XR].h, 16 * (t // XR + 1))
                v.tensor_reduce(xmax[:, t:t + 1], xr[:, t % XR, :], AX.X, ALU.max,
                                apply_absolute_value=True).then_inc(amaxed.h, 1)
            for i in range(4):
                dve.wait_ge(w_in[i].h, 16)
                v.tensor_reduce(amax[:, 1 + i:2 + i], w32[i], AX.X, ALU.max, apply_absolute_value=True)
            dve.wait_ge(small_in.h, 6 * 16)
            for i in range(2):
                last = v.tensor_reduce(amax[:, 5 + i:6 + i], b_t[:, i, :], AX.X, ALU.max, apply_absolute_value=True)
            link(last)
            dve.wait_ge(amaxed.h, NT)
            v.tensor_reduce(amax[:, 0:1], xmax[:, :], AX.X, ALU.max).then_inc(amaxed.h, 1)
            link(v.memset(att[:, 0, :], 1.0))
            for k in range(KT):
                last = v.tensor_scalar(bv_rep[:, k, :], bv_rep[:, k, :], b_t[:, 2, k:k + 1], None, ALU.mult)
            last.then_inc(bvrep.h, 1)
            dve.wait_ge(gmaxed.h, 1)
            link(v.tensor_scalar(expo[:, :], gmax[:, 1:5].bitcast(I32), 23, None, ALU.logical_shift_right))
            link(v.tensor_scalar(expo[:, :], expo[:, :], -1.0, 268.0, ALU.mult, ALU.add))
            link(v.tensor_scalar(expo[:, :], expo[:, :], 167.0, None, ALU.min))
            link(v.tensor_scalar(sw[:, :].bitcast(I32), expo[:, :], 23, None, ALU.logical_shift_left))
            v.tensor_scalar(c4[:, 1:4], gmax[:, 1:4], float(D), None, ALU.mult)
            v.tensor_copy(d4[:, 1:3], gmax[:, 5:7])
            v.reciprocal(rw[:, :], sw[:, :]).then_inc(dconst.h, 1)
            dve.wait_ge(dconst.h, 1)
            for i in range(4):
                dve.wait_ge(whi.h, i + 1)
                v.scalar_tensor_tensor(w_lo[:, i, :, :].rearrange("p k n -> p (k n)"), w32[i], sw[:, i:i + 1],
                                       w_hi[:, i, :, :].rearrange("p k n -> p (k n)"), ALU.mult, ALU.subtract)\
                    .then_inc(wlo.h, 1)
            dve.wait_ge(bvwo.h, 1)
            v.tensor_tensor(bo_b[:, :], op[:, :], bo_b[:, :], ALU.add).then_inc(bo_ready.h, 1)
            dve.sem_inc(masked_n.h, 2)
            dve.sem_inc(ot_l.h, ot_l.credit)
            dve.sem_inc(y_sb.h, y_sb.credit)
            dve.sem_inc(pv.h, pv.credit)
            dve.sem_inc(o_sb.h, o_sb.credit)

            def scales(b):
                links = [0]

                def linkb(ins):
                    links[0] += 1
                    ins.then_inc(dlb.h, 1)
                    dve.wait_ge(dlb.h, dlb.at(b, 1 + links[0]))

                dve.wait_ge(gmaxed.h, gmaxed.at(b, 1))
                linkb(v.scalar_tensor_tensor(bound[:, :], c4[:, :], gmax[:, 0:1], d4[:, :], ALU.mult, ALU.add))
                linkb(v.tensor_scalar(expo[:, :], bound[:, :].bitcast(I32), 23, None, ALU.logical_shift_right))
                linkb(v.tensor_tensor(expo[:, :], target4[:, :], expo[:, :], ALU.subtract))
                linkb(v.tensor_tensor(expo[:, :], expo[:, :], cap4[:, :], ALU.min))
                linkb(v.tensor_scalar(sc[:, :].bitcast(I32), expo[:, :], 23, None, ALU.logical_shift_left))
                v.tensor_scalar(beta_t[:, 0, :], b_t[:, 0, :], sc[:, 1:2], None, ALU.mult)
                v.tensor_scalar(beta_t[:, 1, :], b_t[:, 1, :], sc[:, 2:3], None, ALU.mult)
                linkb(v.reciprocal(rx[:, :], sc[:, 0:1]))
                v.scalar_tensor_tensor(alpha[:, :], sc[:, 1:4], rx[:, :], rw[:, 0:3], ALU.mult, ALU.mult)\
                    .then_inc(scaled.h, 1)

            def mask_rows(b, t):
                for f in range(2):
                    dve.wait_ge(a_in[f].h, a_in[f].at(b, 16 * (t + 1)))
                    v.tensor_scalar(mask_n[:, t, f * HALF:(f + 1) * HALF], ar[:, f, :], 0.0, MASKED,
                                    ALU.is_equal, ALU.mult).then_inc(masked_n.h, 1)

            def x_lo(b, t):
                dve.wait_ge(xt_h.h, xt_h.at(b, t + 1))
                v.scalar_tensor_tensor(xt_lo[:, :, t * P:(t + 1) * P],
                                       mx[:, t % 2, :].rearrange("p (k n) -> p k n", n=P), sc[:, 0:1],
                                       xt_hi[:, :, t * P:(t + 1) * P], ALU.mult, ALU.subtract)\
                    .then_inc(xt_l.h, 1)

            scales(-1)
            for t in range(NT):
                x_lo(-1, t)
                mask_rows(-1, t)

            with dve.Fori(0, B) as b:
                def v_lo(t):
                    dve.wait_ge(v_h.h, v_h.at(b, t + 1))
                    v.scalar_tensor_tensor(vt[:, t, :, 0:HD], og_bank[t % 2].rearrange("p (h d) -> p h d", d=HD),
                                           alpha[:, 2:3], vt[:, t, :, HD:2 * HD], ALU.mult, ALU.subtract)\
                        .then_inc(v_l.h, 1)

                def maxima(h, t):
                    dve.wait_ge(mx_ps.h, mx_ps.at(b, 8 * h + t + 1))
                    dve.sem_inc(dve_wait.h, 1)
                    s2 = mx[:, :, :].rearrange("p a n -> p (a n)")
                    v.tensor_tensor_reduce(out=s2, in0=s2, in1=mask_n[:, t, :], scale=-1.0 / SHIFT_UNIT,
                                           scalar=3.0e38, op0=ALU.add, op1=ALU.min,
                                           accum_out=gam[:, t:t + 1]).then_inc(mx_done.h, 1)

                def shift_lo(h, f):
                    dve.wait_ge(gam_h.h, gam_h.at(b, 2 * h + f + 1))
                    v.tensor_tensor(shl[:, 4 * f:4 * f + 4, 1], gam[:, 4 * f:4 * f + 4],
                                    shl[:, 4 * f:4 * f + 4, 0], ALU.subtract).then_inc(gam_l.h, 1)

                def normalise(u):
                    h, f = u // 2, u % 2
                    dve.wait_ge(pv.h, pv.at(b, 2 * u + 2))
                    dve.wait_ge(o_sb.h, o_sb.at(b, u))
                    o = op[:, 0:4 * OW].rearrange("p (t w) -> p t w", w=OW)
                    v.reciprocal(rinv[:, :], o[:, :, HD]).then_inc(o_inv.h, 1)
                    dve.wait_ge(o_inv.h, o_inv.at(b, u + 1))
                    v.tensor_tensor(att[:, 4 * f:4 * f + 4, h * HD:(h + 1) * HD], o[:, :, 0:HD],
                                    rinv[:, :].unsqueeze(2).to_broadcast([P, 4, HD]), ALU.mult)\
                        .then_inc(o_sb.h, 1)

                dve.wait_ge(scaled.h, scaled.at(b, 0))
                dve.wait_ge(ex_sb.h, ex_sb.at(b, 0))
                v.tensor_scalar(so[:, :], sc[:, 3:4], sw[:, 3:4], None, ALU.mult)
                v.tensor_scalar(sqk[:, :], sc[:, 1:2], sc[:, 2:3], float(HD) ** 0.5, ALU.mult, ALU.mult)\
                    .then_inc(dlb.h, 1)
                dve.wait_ge(dlb.h, dlb.at(b, 1))
                v.reciprocal(gsc[:, :], sqk[:, :])
                v.reciprocal(ao[:, :], so[:, :])
                v.tensor_scalar(shl[:, :, 2], ones8[:, :], sqk[:, :], LN64 / SHIFT_UNIT,
                                ALU.mult, ALU.mult).then_inc(rescaled.h, 1)
                for t in range(4):
                    v_lo(t)
                for t in range(4):
                    maxima(0, t)
                shift_lo(0, 0)
                for t in range(4, NT):
                    v_lo(t)
                    maxima(0, t)
                for h, s in STEPS:
                    c, u = 8 * h + s, 2 * h + s // 4
                    if s % 4 == 0 and u >= 2:
                        normalise(u - 2)
                    dve.wait_ge(st_ps.h, st_ps.at(b, c + 1))
                    f, i = s // 4, s % 4
                    chunk = st[c % 2][:, :, :]
                    v.scalar_tensor_tensor(chunk, mask_t[:, 2 * i:2 * i + 2, f * HALF:(f + 1) * HALF], MASKED,
                                           chunk, ALU.mult, ALU.add).then_inc(st_mk.h, 1)
                    if h < H - 1:
                        maxima(h + 1, s)
                    if s == 0:
                        shift_lo(h, 1)
                    if s == 4 and h < H - 1:
                        shift_lo(h + 1, 0)
                    t = max_tile(h, s)
                    if t is not None:
                        dve.wait_ge(x_in[t % XR].h, x_in[t % XR].at(b, 16 * (t // XR + 1)))
                        v.tensor_reduce(xmax[:, t:t + 1], xr[:, t % XR, :], AX.X, ALU.max,
                                        apply_absolute_value=True).then_inc(xmaxed.h, 1)
                    if (h, s) == (4, 0):
                        dve.wait_ge(xmaxed.h, xmaxed.at(b, NT))
                        v.tensor_reduce(amax[:, 0:1], xmax[:, :], AX.X, ALU.max).then_inc(xm_all.h, 1)
                    if (h, s) == (5, 4):
                        dve.wait_ge(grp32.h, grp32.at(b, 4 * PAIRS))
                        scales(b)
                    if h == H - 1:
                        if s:
                            x_lo(b, s - 1)
                        mask_rows(b, s)
                normalise(2 * H - 2)
                x_lo(b, NT - 1)
                def att_lo(t):
                    dve.wait_ge(ot_h.h, ot_h.at(b, t + 1))
                    v.tensor_tensor(ot_lo[t % 4], mx[:, t % 2, :].rearrange("p (k n) -> p k n", n=P),
                                    ot_hi[t % 4], ALU.subtract).then_inc(ot_l.h, 1)

                att_lo(0)
                att_lo(1)
                normalise(2 * H - 1)
                for t in range(NT + 1):
                    if t < NT:
                        dve.wait_ge(z_ps.h, z_ps.at(b, t + 1))
                        dve.wait_ge(xb.h, xb.at(b, t + 1))
                        dve.wait_ge(y_out[t % 4].h, y_out[t % 4].at(b, 16 * (t // 4)))
                        v.scalar_tensor_tensor(yr[:, t % 4, :], st_bank[t % 4], ao[:, :],
                                               xr[:, (2 * NT + t) % XR, :], ALU.mult, ALU.add).then_inc(y_sb.h, 1)
                    if t + 2 < NT:
                        att_lo(t + 2)
                    if t < NT:
                        dve.wait_ge(y_sb.h, y_sb.at(b, t + 1))
                        v.bn_stats(stats[:, t % 2, :], yr[:, t % 4, :]).then_inc(y_st.h, 1)
                    if t >= 1:
                        z = t - 1
                        dve.wait_ge(y_mv.h, y_mv.at(b, z + 1))
                        v.scalar_tensor_tensor(yr[:, z % 4, :], yr[:, z % 4, :], mv[:, z % 2, 0:1], gamma_b[:, :],
                                               ALU.subtract, ALU.mult).then_inc(y_ga.h, 1)
                    if t < NT:
                        dve.wait_ge(y_st.h, y_st.at(b, t + 1))
                        dve.sem_inc(dve_wait.h, 1)
                        v.bn_aggr(mv[:, t % 2, :], stats[:, t % 2, :]).then_inc(y_mv.h, 1)
                    if t >= 1:
                        z = t - 1
                        dve.wait_ge(y_ga.h, y_ga.at(b, z + 1))
                        dve.wait_ge(y_rs.h, y_rs.at(b, z + 1))
                        v.scalar_tensor_tensor(yr[:, z % 4, :], yr[:, z % 4, :], rstd[:, z % 2:z % 2 + 1],
                                               beta_b[:, :], ALU.mult, ALU.add).then_inc(y_be.h, 1)

        @block.gpsimd
        def _(pool):
            g = nc.gpsimd
            for m in (id32, id16, idbf):
                g.memset(m[:, :], 0.0).then_inc(zeroed.h, 1)
            pool.wait_ge(zeroed.h, 3)
            for m in (id32, id16, idbf):
                g.affine_select(out=m[:, :], in_=m[:, :], compare_op=ALU.not_equal, fill=1.0, base=0,
                                pattern=[[-1, P]], channel_multiplier=1).then_inc(consts.h, 1)
            pool.wait_ge(amaxed.h, NT + 1)
            g.partition_all_reduce(gmax[:, :], amax[:, :], P, ABSMAX).then_inc(gmaxed.h, 1)
            pool.sem_inc(grp_l.h, grp_l.credit)
            pool.sem_inc(p_l.h, p_l.credit)

            with pool.Fori(0, B) as b:
                def group_lo(gr):
                    w, f = GROUPS[gr % 4]
                    which = 1 - w
                    pool.wait_ge(grp_h.h, grp_h.at(b, gr + 1))
                    part = stage[:, which, :, f * HALF:(f + 1) * HALF]
                    g.tensor_tensor(part[:, 1, :], proj[:, gr % 2, :], part[:, 0, :], ALU.subtract)\
                        .then_inc(grp_l.h, 1)

                for gr in range(8):
                    group_lo(gr)
                for h, s in STEPS:
                    c, u = 8 * h + s, 2 * h + s // 4
                    pool.wait_ge(p_h.h, p_h.at(b, c + 1))
                    m = slice(2 * (s % 4), 2 * (s % 4) + 2)
                    g.tensor_tensor(pr_lo[u % 2][:, m, :].rearrange("p a n -> p (a n)"), ex[:, c % 2, :],
                                    pr_hi[u % 2][:, m, :].rearrange("p a n -> p (a n)"), ALU.subtract)\
                        .then_inc(p_l.h, 1)
                    if s % 4 == 0 and u and group_of((u - 1) // 2, 0 if u % 2 else 4) is not None:
                        group_lo(group_of((u - 1) // 2, 0 if u % 2 else 4))
                    if (h, s) == (4, 6):
                        pool.wait_ge(xm_all.h, xm_all.at(b, 1))
                        pool.wait_ge(scaled.h, scaled.at(b, 0))
                        pool.sem_inc(pool_wait.h, 1)
                        g.partition_all_reduce(gmax[:, 0:1], amax[:, 0:1], P, ABSMAX).then_inc(gmaxed.h, 1)
                for t in range(NT + 1):
                    if t < NT:
                        n = 2 * NT + t
                        pool.wait_ge(x_in[n % XR].h, x_in[n % XR].at(b, 16 * (n // XR + 1)))
                        g.tensor_tensor(xr[:, n % XR, :], xr[:, n % XR, :], bo_b[:, :], ALU.add).then_inc(xb.h, 1)
                    if t >= 1:
                        z = t - 1
                        pool.wait_ge(y_mv.h, y_mv.at(b, z + 1))
                        g.tensor_tensor(vpe[:, z % 2:z % 2 + 1], mv[:, z % 2, 1:2], eps[:, :], ALU.add)\
                            .then_inc(y_ve.h, 1)
                        pool.wait_ge(y_ve.h, y_ve.at(b, z + 1))
                        g.tensor_tensor(rstd[:, z % 2:z % 2 + 1], vpe[:, z % 2:z % 2 + 1], mhalf[:, :], ALU.pow)\
                            .then_inc(y_rs.h, 1)


_INS = ['x', 'adj', 'L0_gnn_Wq', 'L0_gnn_bq', 'L0_gnn_Wk', 'L0_gnn_bk', 'L0_gnn_Wv', 'L0_gnn_bv',
        'L0_gnn_Wo', 'L0_gnn_bo', 'L0_gnn_gamma', 'L0_gnn_beta']


def kernel(**inputs):
    import numpy as np
    import concourse.bacc as bacc
    from concourse.bass_utils import run_bass_kernel_spmd

    nc = bacc.Bacc("TRN2", target_bir_lowering=False, num_devices=1)
    arrays, args = {}, []
    for name in _INS:
        a = np.ascontiguousarray(inputs[name])
        arrays[f"in_{name}"] = a
        args.append(nc.dram_tensor(f"in_{name}", a.shape, mybir.dt.from_np(a.dtype), kind="ExternalInput").ap())
    out = nc.dram_tensor("result", inputs["x"].shape, F32, kind="ExternalOutput").ap()
    gnn_attention(nc, *args, out)
    r = run_bass_kernel_spmd(nc, [arrays], core_ids=[0])
    return r.results[0]["result"]
```

```python
from contextlib import ExitStack

import concourse.bass as bass
from concourse import mybir

F32 = mybir.dt.float32
F16 = mybir.dt.float16
BF16 = mybir.dt.bfloat16
I32 = mybir.dt.int32
U8 = mybir.dt.uint8
ALU = mybir.AluOpType
ACT = mybir.ActivationFunctionType
AX = mybir.AxisListType
ABSMAX = bass.bass_isa.ReduceOp.absmax

P = 128
HALF = 512
MASKED = -(2.0 ** 100)
SHIFT_UNIT = 2.0 ** 15
LN64 = 4.1588830833596715
EPS = 1e-5


class Sem:

    def __init__(self, handle, per, credit=0):
        self.h, self.per, self.credit = handle, per, credit

    def at(self, b, k):
        return b * self.per + (self.credit + k)


def gnn_attention(nc, x, adj, Wq, bq, Wk, bk, Wv, bv, Wo, bo, gamma, beta, out):
    B, N, D = x.shape
    H = 8
    HD = D // H
    NT = N // P
    KT = D // P
    PAIRS = H // 2
    CHUNKS = H * 2 * (NT // 2)
    VW = 2 * HD + 2
    OW = HD + 1
    XR = 3
    XT = 3 * NT
    assert HD == 64 and NT == 8 and KT == 4 and XT % XR == 0

    ctx = ExitStack()
    with ctx:
        def sb(name, shape, dt):
            return ctx.enter_context(nc.sbuf_tensor(name, shape, dt))

        def ps(name, shape, dt):
            return ctx.enter_context(nc.psum_tensor(name, shape, dt))

        def sem(name, per=0, credit=0):
            return Sem(ctx.enter_context(nc.semaphore(name)), per, credit)

        w_hi = sb("w_hi", [P, 4, KT, D], F16)
        w_lo = sb("w_lo", [P, 4, KT, D], F16)
        xt_hi = sb("xt_hi", [P, KT, N], F16)
        xt_lo = sb("xt_lo", [P, KT, N], F16)
        q1 = [sb(f"q1_{i}", [P, N], F16) for i in range(4)]
        q2 = [sb(f"q2_{i}", [P, N], F16) for i in range(4)]
        k1 = [sb(f"k1_{i}", [P, N], F16) for i in range(4)]
        k2 = [sb(f"k2_{i}", [P, N], F16) for i in range(4)]
        stage = sb("stage", [P, 2, 2, N], F16)
        proj = sb("proj", [P, 2, HALF], F32)
        vt = sb("vt", [P, NT, H, VW], F16)
        mask_n = sb("mask_n", [P, NT, N], BF16)
        mask_t = sb("mask_t", [P, NT, N], U8)
        ex = sb("ex", [P, 2, N], F32)
        pr_hi = [sb(f"pr_hi{i}", [P, NT, HALF], F16) for i in range(2)]
        pr_lo = [sb(f"pr_lo{i}", [P, NT, HALF], F16) for i in range(2)]
        att = sb("att", [P, NT, D], F32)
        xr = sb("xr", [P, XR, D], F32)
        ar = sb("ar", [P, 2, HALF], I32)
        gamma_b = sb("gamma_b", [P, D], F32)
        beta_b = sb("beta_b", [P, D], F32)
        bo_b = sb("bo_b", [P, D], F32)
        id32 = sb("id32", [P, P], F32)
        id16 = sb("id16", [P, P], F16)
        idbf = sb("idbf", [P, P], BF16)
        b_t = sb("b_t", [P, 3, KT], F32)
        beta_t = sb("beta_t", [P, 2, KT], F32)
        amax = sb("amax", [P, 8], F32)
        xmax = sb("xmax", [P, NT], F32)
        gmax = sb("gmax", [P, 8], F32)
        sw = sb("sw", [P, 4], F32)
        rw = sb("rw", [P, 4], F32)
        c4 = sb("c4", [P, 4], F32)
        d4 = sb("d4", [P, 4], F32)
        target4 = sb("target4", [P, 4], F32)
        cap4 = sb("cap4", [P, 4], F32)
        bound = sb("bound", [P, 4], F32)
        expo = sb("expo", [P, 4], I32)
        sc = sb("sc", [P, 4], F32)
        rx = sb("rx", [P, 1], F32)
        alpha = sb("alpha", [P, 3], F32)
        sqk = sb("sqk", [P, 1], F32)
        gsc = sb("gsc", [P, 1], F32)
        so = sb("so", [P, 1], F32)
        ao = sb("ao", [P, 1], F32)
        ones8 = sb("ones8", [P, NT], F32)
        gam = sb("gam", [P, NT], F32)
        shl = sb("shl", [P, NT, 32], F16)
        rinv = sb("rinv", [P, NT // 2], F32)
        stats = sb("stats", [P, 2, 6], F32)
        mv = sb("mv", [P, 2, 2], F32)
        vpe = sb("vpe", [P, 2], F32)
        rstd = sb("rstd", [P, 2], F32)
        mhalf = sb("mhalf", [P, 1], F32)
        eps = sb("eps", [P, 1], F32)
        yr = ex[:, :, :].rearrange("p a (c n) -> p (a c) n", n=D)
        ot_hi, ot_lo = [[t[:, i, :].rearrange("p (k n) -> p k n", n=P) for i in range(4)]
                        for t in (pr_hi[0], pr_lo[0])]
        ar_ring = [ar[:, 0, :], ar[:, 1, :], q1[2][:, :].bitcast(I32), k1[2][:, :].bitcast(I32)]
        w32 = [t[:, :, :].rearrange("p a n -> p (a n)").bitcast(F32)
               for t in (pr_hi[0], pr_hi[1], pr_lo[0], pr_lo[1])]
        bv_rep = att[:, 0, :].rearrange("p (k n) -> p k n", n=P)

        st = [ps(f"st{i}", [P, 2, HALF], F32) for i in range(2)]
        mx = ps("mx", [P, 2, HALF], F32)
        op = ps("op", [P, HALF], F32)
        gp = ps("gp", [P, HALF], F32)
        st_bank = [st[i // 2][:, i % 2, :] for i in range(4)]
        og_bank = [op[:, :], gp[:, :]]
        mx_bf = mx[:, :, :].rearrange("p a n -> p (a n)").bitcast(BF16).rearrange("p (a t n) -> p a t n", a=2, n=P)
        st_bf = [t.bitcast(BF16).rearrange("p (t n) -> p t n", n=P) for t in st_bank]

        w_in = [sem(f"w_in{i}") for i in range(4)]
        small_in = sem("small_in")
        rows_in = sem("rows_in")
        x_in = [sem(f"x_in{i}", 16 * XT // XR, 16 * ((2 * NT - 1 - i) // XR + 1)) for i in range(XR)]
        a_in = [sem(f"a_in{i}", 16 * NT // 2, 16 * NT // 2) for i in range(4)]
        k_in = [sem(f"k_in{i}", 2 * 48, 48 if i < 2 else 0) for i in range(4)]
        q_in = [sem(f"q_in{i}", 2 * 48, 48 if i < 2 else 0) for i in range(4)]
        y_out = [sem(f"y_out{i}", 2 * 16, 16) for i in range(4)]
        zeroed = sem("zeroed")
        fixed = sem("fixed")
        consts = sem("consts")
        dconst = sem("dconst")
        amaxed = sem("amaxed")
        gmaxed = sem("gmaxed", 1, 1)
        whi = sem("whi")
        wlo = sem("wlo")
        bvrep = sem("bvrep")
        bvwo = sem("bvwo")
        bo_ready = sem("bo_ready")
        scaled = sem("scaled", 1, 1)
        rescaled = sem("rescaled", 1)
        dl = sem("dl")
        dlb = sem("dlb", 7, 6)
        dve_wait = sem("dve_wait")
        pool_wait = sem("pool_wait")
        sp_wait = sem("sp_wait")
        masked_n = sem("masked_n", 2 * NT, 2 * NT + 4)
        xt_ps = sem("xt_ps", NT, NT)
        xt_h = sem("xt_h", NT, NT)
        xt_l = sem("xt_l", NT, NT)
        mt_ps = sem("mt_ps", NT, NT)
        mt_sb = [sem(f"mt_sb{i}", NT // 2, NT // 2) for i in range(2)]
        grp = sem("grp", 4 * PAIRS, 4)
        grp32 = sem("grp32", 4 * PAIRS, 4)
        grp_h = sem("grp_h", 4 * PAIRS, 4)
        grp_l = sem("grp_l", 4 * PAIRS, 6)
        v_ps = sem("v_ps", NT)
        v_h = sem("v_h", NT)
        v_l = sem("v_l", NT)
        mx_ps = sem("mx_ps", CHUNKS)
        mx_done = sem("mx_done", CHUNKS)
        gam_h = sem("gam_h", 2 * H)
        gam_l = sem("gam_l", 2 * H)
        sh_ps = sem("sh_ps", 2 * H, 2)
        sh_sb = sem("sh_sb", 2 * H)
        st_ps = sem("st_ps", CHUNKS)
        st_mk = sem("st_mk", CHUNKS)
        ex_sb = sem("ex_sb", CHUNKS, 1)
        p_h = sem("p_h", CHUNKS, 2)
        p_l = sem("p_l", CHUNKS, 2)
        pv = sem("pv", 4 * H, 4)
        o_inv = sem("o_inv", 2 * H)
        o_sb = sem("o_sb", 2 * H, 1)
        xmaxed = sem("xmaxed", NT)
        xm_all = sem("xm_all", 1)
        ot_ps = sem("ot_ps", NT)
        ot_h = sem("ot_h", NT, 1)
        ot_l = sem("ot_l", NT, 1)
        z_ps = sem("z_ps", NT)
        xb = sem("xb", NT)
        y_sb = sem("y_sb", NT, 4)
        y_st = sem("y_st", NT)
        y_mv = sem("y_mv", NT)
        y_ve = sem("y_ve", NT)
        y_rs = sem("y_rs", NT)
        y_ga = sem("y_ga", NT)
        y_be = sem("y_be", NT)

        GROUPS = [(w, f) for w in (1, 0) for f in range(2)]

        def pair_of(g):
            return (g // 4 + 1) % PAIRS

        def arrived(h):
            return 48 * ((h + 2) // 4)

        def slot(h):
            return h % 4

        def own(h):
            a = HD * (h % 2)
            return slice(a, a + HD), slice(HD - a, 2 * HD - a)

        def shift_rows(h):
            a = HD * (1 - h % 2)
            return slice(a, a + 32)

        STEPS = [(h, s) for h in range(H) for s in range(8)]
        PROJECT = {0: (2, 0), 1: (2, 6), 2: (3, 0), 3: (3, 6)}
        TO_F32, TO_HI, TO_LO = {1: 2, 3: 3}, {2: 2, 3: 3}, {3: 2, 4: 3}
        for unit, g in [(unit, 3 + unit) for unit in range(1, 9)] + [(g, g) for g in range(12, 16)]:
            PROJECT[4 * unit], PROJECT[4 * unit + 1] = (g, 0), (g, 6)
            TO_F32[4 * unit + 1] = TO_HI[4 * unit + 2] = TO_LO[4 * unit + 3] = g
        del TO_F32[CHUNKS - 3], TO_HI[CHUNKS - 2], TO_LO[CHUNKS - 5], TO_LO[CHUNKS - 1]
        X_HEAD = 5

        def mt_bank(t):
            return mx_bf[:, t % 2, :, :] if t < 4 else st_bf[t - 4]

        def in_batch(b):
            return not (isinstance(b, int) and b == -1)

        block = ctx.enter_context(nc.Block())

        @block.sync
        def _(sp):
            def load_w(i):
                sp.dma_start(w32[i].rearrange("p (k n) -> p k n", n=D),
                             (Wq, Wk, Wv, Wo)[i].rearrange("(k p) n -> p k n", p=P)).then_inc(w_in[i].h, 16)

            for n in range(2 * NT):
                t = n % NT
                if XR <= n < NT + XR:
                    sp.wait_ge(amaxed.h, n - XR + 1)
                if n >= NT + XR:
                    sp.wait_ge(xt_ps.h, xt_ps.at(-1, t - XR + 1))
                sp.dma_start(xr[:, n % XR, :], x[0, t * P:(t + 1) * P, :]).then_inc(x_in[n % XR].h, 16)
                if n == 2:
                    load_w(0)
                    with nc.allow_non_contiguous_dma(reason="biases by feature, once"):
                        for i, v in enumerate((bq, bk, bv)):
                            sp.dma_start(b_t[:, i, :], v.rearrange("(k p) -> p k", p=P)).then_inc(small_in.h, 16)
                if 3 <= n < 6:
                    load_w(n - 2)
                if n == NT:
                    for row, v in ((gamma_b, gamma), (beta_b, beta), (bo_b, bo)):
                        sp.dma_start(row[:, :], v.partition_broadcast(P)).then_inc(rows_in.h, 16)
                if n >= NT:
                    for i in (2 * t, 2 * t + 1):
                        if t >= 2:
                            sp.wait_ge(masked_n.h, masked_n.at(-1, i - 3))
                        sp.dma_start(ar_ring[i % 4], adj[0, t * P:(t + 1) * P, i % 2 * HALF:(i % 2 + 1) * HALF])\
                            .then_inc(a_in[i % 4].h, 16)
            sp.wait_ge(xt_ps.h, xt_ps.at(-1, NT))

            def arrange(h, which):
                src, far = own(h)
                hi, lo = stage[src, which, 0, :], stage[src, which, 1, :]
                if which == 0:
                    places, done = ((k1[slot(h)][src, :], hi), (k1[slot(h)][far, :], hi),
                                    (k2[slot(h)][src, :], lo)), k_in[slot(h)]
                else:
                    places, done = ((q1[slot(h)][src, :], hi), (q1[slot(h)][far, :], lo),
                                    (q2[slot(h)][src, :], hi)), q_in[slot(h)]
                for dst, part in places:
                    sp.dma_start(dst, part).then_inc(done.h, 16)

            sp.wait_ge(zeroed.h, 3 + 8)
            for which in range(2):
                sp.wait_ge(grp_l.h, grp_l.at(-1, 14 + 2 * which))
                for h in range(2):
                    arrange(h, which)

            for i in range(4):
                sp.sem_inc(y_out[i].h, y_out[i].credit)

            with sp.Fori(0, B) as b:
                def load_x(n, batch, t):
                    sp.dma_start(xr[:, n % XR, :], x[batch, t * P:(t + 1) * P, :]).then_inc(x_in[n % XR].h, 16)

                nxt = (b + 1) % B

                def max_load(t):
                    if t < XR:
                        sp.wait_ge(y_sb.h, y_sb.at(b, t - XR + 1))
                    else:
                        sp.wait_ge(xmaxed.h, xmaxed.at(b, t - XR + 1))
                    load_x(t, nxt, t)

                def transpose_load(t):
                    if t < XR:
                        sp.wait_ge(xmaxed.h, xmaxed.at(b, NT - XR + t + 1))
                    else:
                        sp.wait_ge(xt_ps.h, xt_ps.at(b, t - XR + 1))
                    load_x(NT + t, nxt, t)

                def residual_load(t):
                    if t < XR:
                        sp.wait_ge(xt_ps.h, xt_ps.at(b, NT - XR + t + 1))
                    else:
                        sp.wait_ge(y_sb.h, y_sb.at(b, t - XR + 1))
                    load_x(2 * NT + t, b, t)

                def write_rows(t):
                    sp.wait_ge(y_be.h, y_be.at(b, t + 1))
                    sp.dma_start(out[b, t * P:(t + 1) * P, :], yr[:, t % 4, :]).then_inc(y_out[t % 4].h, 16)

                def adjacency_load(t):
                    if t == 1:
                        sp.wait_ge(st_ps.h, st_ps.at(b, 56))
                    for i in (2 * t, 2 * t + 1):
                        if t != 1:
                            sp.wait_ge(masked_n.h, masked_n.at(b, i - 3))
                        sp.dma_start(ar_ring[i % 4], adj[nxt, t * P:(t + 1) * P, i % 2 * HALF:(i % 2 + 1) * HALF])\
                            .then_inc(a_in[i % 4].h, 16)

                for t in range(XR):
                    max_load(t)
                sp.wait_ge(masked_n.h, masked_n.at(b, 0))
                sp.sem_inc(sp_wait.h, 1)
                sp.wait_ge(grp_l.h, grp_l.at(b, 2))
                arrange(2, 0)
                arrange(3, 0)
                for t in range(XR, NT):
                    max_load(t)
                sp.wait_ge(grp_l.h, grp_l.at(b, 4))
                arrange(2, 1)
                arrange(3, 1)
                sp.wait_ge(grp_l.h, grp_l.at(b, 6))
                sp.sem_inc(sp_wait.h, 1)
                sp.wait_ge(st_ps.h, st_ps.at(b, 8))
                arrange(4, 0)
                sp.wait_ge(grp_l.h, grp_l.at(b, 8))
                arrange(4, 1)
                sp.wait_ge(st_ps.h, st_ps.at(b, 16))
                arrange(5, 0)
                arrange(5, 1)
                transpose_load(0)
                transpose_load(1)
                adjacency_load(0)
                sp.wait_ge(grp_l.h, grp_l.at(b, 10))
                sp.sem_inc(sp_wait.h, 1)
                sp.wait_ge(st_ps.h, st_ps.at(b, 24))
                arrange(6, 0)
                transpose_load(2)
                sp.wait_ge(grp_l.h, grp_l.at(b, 12))
                arrange(6, 1)
                sp.wait_ge(st_ps.h, st_ps.at(b, 32))
                arrange(7, 0)
                arrange(7, 1)
                for t in range(XR, NT):
                    transpose_load(t)
                for t in range(XR):
                    residual_load(t)
                for t in range(1, NT):
                    adjacency_load(t)
                sp.wait_ge(grp_l.h, grp_l.at(b, 14))
                sp.sem_inc(sp_wait.h, 1)
                sp.wait_ge(st_ps.h, st_ps.at(b, 48))
                arrange(0, 0)
                arrange(1, 0)
                sp.wait_ge(grp_l.h, grp_l.at(b, 16))
                arrange(0, 1)
                arrange(1, 1)
                for t in range(XR, NT):
                    residual_load(t)
                    if t >= 4:
                        write_rows(t - 4)
                for t in range(NT - 4, NT):
                    write_rows(t)
            for i in range(4):
                sp.wait_ge(y_out[i].h, y_out[i].at(B, 0))

        @block.tensor
        def _(pe):
            mm = nc.tensor.matmul
            pe.sem_inc(sh_ps.h, sh_ps.credit)
            pe.wait_ge(consts.h, 3)

            def x_transpose(b, t, loads_before):
                n = NT + t
                pe.wait_ge(x_in[n % XR].h, loads_before + 16 * (n // XR + 1))
                if t:
                    pe.wait_ge(xt_h.h, xt_h.at(b, t))
                    pe.wait_ge(xt_l.h, xt_l.at(b, t))
                elif in_batch(b):
                    pe.wait_ge(grp32.h, grp32.at(b, 12))
                for k in range(KT):
                    last = mm(gp[:, k * P:(k + 1) * P], xr[:, n % XR, k * P:(k + 1) * P],
                              id32[:, :], is_transpose=True, start=True, stop=True)
                last.then_inc(xt_ps.h, 1)

            def mask_transpose(b, t):
                pe.wait_ge(masked_n.h, masked_n.at(b, 2 * t + 2))
                if 2 <= t < 4:
                    pe.wait_ge(mt_sb[t % 2].h, mt_sb[t % 2].at(b, 1))
                elif t < 2 and in_batch(b):
                    pe.wait_ge(mx_done.h, mx_done.at(b, CHUNKS))
                elif t >= 4 and in_batch(b):
                    pe.wait_ge(ex_sb.h, ex_sb.at(b, CHUNKS - 1 + (t - 4) // 2))
                for m in range(NT):
                    last = mm(mt_bank(t)[:, m, :], mask_n[:, t, m * P:(m + 1) * P], idbf[:, :],
                              is_transpose=True, start=True, stop=True)
                last.then_inc(mt_ps.h, 1)

            def group(b, g, bank, parts=range(12)):
                w, f = GROUPS[g % 4]
                cols = slice(pair_of(g) * P, (pair_of(g) + 1) * P)
                steps = [(a, c, k) for a, c in ((w_hi, xt_hi), (w_hi, xt_lo), (w_lo, xt_hi)) for k in range(KT)]
                if parts[0] == 0 and g >= 2:
                    if g == 2:
                        pe.wait_ge(v_l.h, v_l.at(b, NT))
                    elif g == 3:
                        pe.wait_ge(sh_sb.h, sh_sb.at(b, 2))
                    elif g == 12:
                        pe.wait_ge(xt_h.h, xt_h.at(b, NT))
                        pe.wait_ge(xt_l.h, xt_l.at(b, NT))
                    elif g == 4:
                        pe.wait_ge(grp32.h, grp32.at(b, 3))
                    else:
                        pe.wait_ge(grp32.h, grp32.at(b, g))
                for n in parts:
                    a, c, k = steps[n]
                    last = mm(bank, a[:, w, k, cols], c[:, k, f * HALF:(f + 1) * HALF],
                              start=(n == 0), stop=(n == 3 * KT - 1))
                if parts[-1] == 3 * KT - 1:
                    last.then_inc(grp.h, 1)

            for t in range(NT):
                x_transpose(-1, t, 0)
            for t in range(NT):
                mask_transpose(-1, t)
            pe.wait_ge(bvrep.h, 1)
            pe.wait_ge(w_in[3].h, 16)
            for k in range(KT):
                last = mm(op[:, :], bv_rep[:, k, :], w32[3][:, k * D:(k + 1) * D], start=(k == 0), stop=(k == KT - 1))
            last.then_inc(bvwo.h, 1)
            pe.wait_ge(whi.h, 4)
            pe.wait_ge(wlo.h, 4)
            for g in range(12, 16):
                group(-1, g, gp[:, :])

            pe.wait_ge(bo_ready.h, 1)
            pe.wait_ge(fixed.h, 1)

            with pe.Fori(0, B) as b:
                def v_tile(t):
                    if t < 2:
                        pe.wait_ge(o_sb.h, o_sb.at(b, 0))
                        pe.wait_ge(grp32.h, grp32.at(b, 0))
                    else:
                        pe.wait_ge(v_l.h, v_l.at(b, t - 1))
                    n = 0
                    for a, c in ((xt_hi, w_hi), (xt_hi, w_lo), (xt_lo, w_hi)):
                        for k in range(KT):
                            last = mm(og_bank[t % 2], a[:, k, t * P:(t + 1) * P], c[:, 2, k, :],
                                      start=(n == 0), stop=(n == 3 * KT - 1))
                            n += 1
                    last.then_inc(v_ps.h, 1)

                def maxima(h, t):
                    if t == 0:
                        pe.wait_ge(k_in[slot(h)].h, k_in[slot(h)].at(b, arrived(h)))
                        pe.wait_ge(q_in[slot(h)].h, q_in[slot(h)].at(b, arrived(h)))
                    if h == 0 and t == 0:
                        pe.wait_ge(ot_l.h, ot_l.at(b, 0))
                        pe.wait_ge(ot_h.h, ot_h.at(b, 0))
                    else:
                        pe.wait_ge(mx_done.h, mx_done.at(b, 8 * h + t))
                    for f in range(2):
                        last = mm(mx[:, f, :], q1[slot(h)][:, t * P:(t + 1) * P],
                                  k1[slot(h)][:, f * HALF:(f + 1) * HALF], start=True, stop=True)
                    last.then_inc(mx_ps.h, 1)

                def shift(h, f):
                    pe.wait_ge(gam_l.h, gam_l.at(b, 2 * h + f + 1))
                    if h == 0 and f == 0:
                        pe.wait_ge(v_l.h, v_l.at(b, NT - 1))
                    elif h == 0:
                        pe.wait_ge(sh_sb.h, sh_sb.at(b, 1))
                    elif (h, f) == (1, 0):
                        pe.wait_ge(grp32.h, grp32.at(b, 4))
                    else:
                        pe.wait_ge(o_sb.h, o_sb.at(b, 2 * h + f - 2))
                    for t in range(4):
                        last = mm(op[shift_rows(h), t * P:(t + 1) * P], shl[:, 4 * f + t, :], id16[:, :],
                                  start=True, stop=True)
                    last.then_inc(sh_ps.h, 1)

                def chunk(h, s):
                    c = 8 * h + s
                    f, i = s // 4, s % 4
                    if c == 0:
                        pe.wait_ge(grp32.h, grp32.at(b, 2))
                    elif c == 1:
                        pe.wait_ge(y_sb.h, y_sb.at(b, 0))
                    else:
                        pe.wait_ge(ex_sb.h, ex_sb.at(b, c - 1))
                    if i == 0:
                        pe.wait_ge(sh_sb.h, sh_sb.at(b, 2 * h + f + 1))
                    n = slice(f * HALF, (f + 1) * HALF)
                    for a in range(2):
                        m = slice((2 * i + a) * P, (2 * i + a + 1) * P)
                        mm(st[c % 2][:, a, :], k1[slot(h)][:, m], q1[slot(h)][:, n], start=True, stop=False)
                        last = mm(st[c % 2][:, a, :], k2[slot(h)][:, m], q2[slot(h)][:, n], start=False, stop=True)
                    last.then_inc(st_ps.h, 1)

                def values(u, part):
                    h = u // 2
                    if part == 0:
                        pe.wait_ge(p_h.h, p_h.at(b, 4 * u + 4))
                        pe.wait_ge(p_l.h, p_l.at(b, 4 * u + 4))
                        pe.wait_ge(sh_sb.h, sh_sb.at(b, min(u + 3, 2 * H)))
                        pe.wait_ge(o_sb.h, o_sb.at(b, u))
                    for t in (2 * part, 2 * part + 1):
                        n = slice(t * P, (t + 1) * P)
                        o = op[:, t * OW:(t + 1) * OW]
                        for m in range(NT):
                            mm(o, pr_hi[u % 2][:, m, n], vt[:, m, h, HD:2 * HD + 1], start=(m == 0), stop=False)
                            mm(o[:, 0:HD], pr_hi[u % 2][:, m, n], vt[:, m, h, 0:HD], start=False, stop=False)
                            last = mm(o, pr_lo[u % 2][:, m, n], vt[:, m, h, HD:2 * HD + 1],
                                      start=False, stop=(m == NT - 1))
                    last.then_inc(pv.h, 1)

                for i in range(2):
                    pe.wait_ge(mt_sb[i].h, mt_sb[i].at(b, 0))
                for g in range(2):
                    pe.wait_ge(y_sb.h, y_sb.at(b, g - 3))
                    group(b, g, st_bank[g])
                for t in range(NT):
                    v_tile(t)
                    if t == NT - 1:
                        shift(0, 0)
                    maxima(0, t)
                for h, s in STEPS:
                    c, u = 8 * h + s, 2 * h + s // 4
                    chunk(h, s)
                    if h == X_HEAD:
                        x_transpose(b, s, x_in[(NT + s) % XR].at(b, 0))
                    if h < H - 1:
                        maxima(h + 1, s)
                    if s == 1:
                        shift(h, 1)
                    if s == 5 and h < H - 1:
                        shift(h + 1, 0)
                    if s % 4 >= 2 and u >= 1:
                        values(u - 1, s % 4 - 2)
                    if c in PROJECT:
                        g, n = PROJECT[c]
                        group(b, g, op[:, :] if g == 3 else gp[:, :], range(n, n + 6))
                    if h == H - 1 and s >= 4:
                        mask_transpose(b, s - 4)
                def att_transpose(t):
                    if t < 2:
                        pe.wait_ge(mt_sb[t].h, mt_sb[t].at(b, 2))
                    else:
                        pe.wait_ge(ot_h.h, ot_h.at(b, t - 1))
                        pe.wait_ge(ot_l.h, ot_l.at(b, t - 1))
                    pe.wait_ge(o_sb.h, o_sb.at(b, 2 * H - 1 + t // 4))
                    for k in range(KT):
                        last = mm(mx[:, t % 2, k * P:(k + 1) * P], att[:, t, k * P:(k + 1) * P],
                                  id32[:, :], is_transpose=True, start=True, stop=True)
                    last.then_inc(ot_ps.h, 1)

                def output(z):
                    if z < 4:
                        pe.wait_ge(mt_sb[z % 2].h, mt_sb[z % 2].at(b, 3 + z // 2))
                    else:
                        pe.wait_ge(y_sb.h, y_sb.at(b, z - 3))
                    pe.wait_ge(ot_h.h, ot_h.at(b, z + 1))
                    pe.wait_ge(ot_l.h, ot_l.at(b, z + 1))
                    n = 0
                    for a, c in ((ot_hi, w_hi), (ot_hi, w_lo), (ot_lo, w_hi)):
                        for k in range(KT):
                            last = mm(st_bank[z % 4], a[z % 4][:, k, :], c[:, 3, k, :],
                                      start=(n == 0), stop=(n == 3 * KT - 1))
                            n += 1
                    last.then_inc(z_ps.h, 1)

                for t in range(4, NT):
                    mask_transpose(b, t)
                att_transpose(0)
                att_transpose(1)
                for part in range(2):
                    values(2 * H - 1, part)
                for t in range(NT):
                    output(t)
                    if t + 2 < NT:
                        att_transpose(t + 2)

        @block.scalar
        def _(act):
            a = nc.scalar.activation
            act.sem_inc(ex_sb.h, ex_sb.credit)
            act.sem_inc(p_h.h, p_h.credit)
            act.sem_inc(ot_h.h, ot_h.credit)

            def x_hi(b, t):
                if t == 0:
                    act.wait_ge(scaled.h, scaled.at(b, 1))
                act.wait_ge(xt_ps.h, xt_ps.at(b, t + 1))
                a(xt_hi[:, :, t * P:(t + 1) * P], gp[:, :].rearrange("p (k n) -> p k n", n=P),
                  ACT.Copy, scale=sc[:, 0:1]).then_inc(xt_h.h, 1)

            def mask_out(b, t):
                act.wait_ge(mt_ps.h, mt_ps.at(b, t + 1))
                a(mask_t[:, :, t * P:(t + 1) * P], mt_bank(t), ACT.Copy, scale=1.0 / MASKED)\
                    .then_inc(mt_sb[0].h, 1)

            for t in range(NT):
                x_hi(-1, t)
                if t % 2:
                    i = t // 2
                    a(w_hi[:, i, :, :].rearrange("p k n -> p (k n)"), w32[i], ACT.Copy, scale=sw[:, i:i + 1])\
                        .then_inc(whi.h, 1)
            act.wait_ge(zeroed.h, 3 + 8)

            def group32(b, g, bank):
                w, _ = GROUPS[g % 4]
                j = pair_of(g)
                act.wait_ge(grp.h, grp.at(b, g + 1))
                act.wait_ge(grp_l.h, grp_l.at(b, g - 1))
                a(proj[:, g % 2, :], bank, ACT.Identity, bias=beta_t[:, w, j:j + 1],
                  scale=alpha[:, w:w + 1]).then_inc(grp32.h, 1)

            def group_hi(b, g):
                w, f = GROUPS[g % 4]
                which = 1 - w
                act.wait_ge(grp32.h, grp32.at(b, g + 1))
                if in_batch(b):
                    for h in (2 * (g // 4), 2 * (g // 4) + 1):
                        done = (k_in, q_in)[which][slot(h)]
                        act.wait_ge(done.h, done.at(b, arrived(h)))
                a(stage[:, which, 0, f * HALF:(f + 1) * HALF], proj[:, g % 2, :], ACT.Copy).then_inc(grp_h.h, 1)

            for t in range(0, NT, 2):
                mask_out(-1, t)
            for g in range(12, 16):
                group32(-1, g, gp[:, :])
                group_hi(-1, g)

            with act.Fori(0, B) as b:
                def shift_hi(h, f):
                    act.wait_ge(mx_done.h, mx_done.at(b, 8 * h + 4 * f + 4))
                    act.wait_ge(sh_ps.h, sh_ps.at(b, 2 * h + f - 1))
                    a(shl[:, 4 * f:4 * f + 4, 0], gam[:, 4 * f:4 * f + 4], ACT.Copy).then_inc(gam_h.h, 1)

                def shift_out(h, f):
                    act.wait_ge(sh_ps.h, sh_ps.at(b, 2 * h + f + 1))
                    a(q2[slot(h)][shift_rows(h), f * HALF:(f + 1) * HALF], op[shift_rows(h), :], ACT.Copy)\
                        .then_inc(sh_sb.h, 1)

                def v_hi(t):
                    act.wait_ge(v_ps.h, v_ps.at(b, t + 1))
                    a(vt[:, t, :, HD:2 * HD], og_bank[t % 2].rearrange("p (h d) -> p h d", d=HD), ACT.Copy,
                      scale=alpha[:, 2:3]).then_inc(v_h.h, 1)

                for g in range(2):
                    group32(b, g, st_bank[g])
                    group_hi(b, g)
                for t in range(NT):
                    if t == NT - 1:
                        shift_out(0, 0)
                    v_hi(t)
                    if t == 3:
                        shift_hi(0, 0)
                for h, s in STEPS:
                    c, u = 8 * h + s, 2 * h + s // 4
                    if s == 0:
                        shift_hi(h, 1)
                    if s == 4 and h < H - 1:
                        shift_hi(h + 1, 0)
                    if s == 1:
                        shift_out(h, 1)
                    if s == 5 and h < H - 1:
                        shift_out(h + 1, 0)
                    if h == X_HEAD:
                        x_hi(b, s)
                    act.wait_ge(st_mk.h, st_mk.at(b, c + 1))
                    act.wait_ge(p_l.h, p_l.at(b, c - 1))
                    act.wait_ge(p_h.h, p_h.at(b, c - 1))
                    if c == 0:
                        act.wait_ge(rescaled.h, rescaled.at(b, 1))
                    if c < 2:
                        for i in (2 * c, 2 * c + 1):
                            act.wait_ge(y_out[i].h, y_out[i].at(b, 0))
                    a(ex[:, c % 2, :], st[c % 2][:, :, :].rearrange("p a n -> p (a n)"), ACT.Exp,
                      scale=gsc[:, 0:1]).then_inc(ex_sb.h, 1)
                    act.wait_ge(ex_sb.h, ex_sb.at(b, c + 1))
                    act.wait_ge(pv.h, pv.at(b, 2 * (u - 1)))
                    a(pr_hi[u % 2][:, 2 * (s % 4):2 * (s % 4) + 2, :].rearrange("p a n -> p (a n)"),
                      ex[:, c % 2, :], ACT.Copy).then_inc(p_h.h, 1)
                    if c in TO_F32:
                        g = TO_F32[c]
                        group32(b, g, op[:, :] if g == 3 else gp[:, :])
                    if c in TO_HI:
                        group_hi(b, TO_HI[c])
                    if c == CHUNKS - 4:
                        mask_out(b, 0)
                    if c == CHUNKS - 1:
                        mask_out(b, 2)
                def att_hi(t):
                    act.wait_ge(ot_ps.h, ot_ps.at(b, t + 1))
                    if t >= 4:
                        act.wait_ge(z_ps.h, z_ps.at(b, t - 3))
                    a(ot_hi[t % 4], mx[:, t % 2, :].rearrange("p (k n) -> p k n", n=P), ACT.Copy)\
                        .then_inc(ot_h.h, 1)

                att_hi(0)
                mask_out(b, 4)
                att_hi(1)
                mask_out(b, 6)
                group32(b, 15, gp[:, :])
                group_hi(b, 15)
                for t in range(2, NT):
                    att_hi(t)

        @block.vector
        def _(dve):
            v = nc.vector
            chain = [0]

            def link(ins):
                chain[0] += 1
                ins.then_inc(dl.h, 1)
                dve.wait_ge(dl.h, chain[0])

            v.memset(vt[:, :, :, 2 * HD:VW].rearrange("p t h w -> p (t h) w"), 1.0)
            v.memset(shl[:, :, :].rearrange("p t n -> p (t n)"), 0.0)
            v.memset(ones8[:, :], 1.0)
            v.memset(mhalf[:, :], -0.5)
            v.memset(eps[:, :], EPS)
            v.memset(amax[:, :], 0.0)
            v.memset(target4[:, :], 268.0)
            v.memset(cap4[:, :], 167.0)
            v.memset(d4[:, :], 0.0)
            v.memset(c4[:, :], 1.0)
            link(v.memset(xmax[:, :], 0.0))
            v.memset(target4[:, 1:3], 265.0)
            v.memset(cap4[:, 1:3], 139.0)
            for t in range(NT):
                dve.wait_ge(x_in[t % XR].h, 16 * (t // XR + 1))
                v.tensor_reduce(xmax[:, t:t + 1], xr[:, t % XR, :], AX.X, ALU.max,
                                apply_absolute_value=True).then_inc(amaxed.h, 1)
                if t >= 4:
                    i = t - 4
                    dve.wait_ge(w_in[i].h, 16)
                    v.tensor_reduce(amax[:, 1 + i:2 + i], w32[i], AX.X, ALU.max, apply_absolute_value=True)
            dve.wait_ge(small_in.h, 3 * 16)
            for i in range(2):
                last = v.tensor_reduce(amax[:, 5 + i:6 + i], b_t[:, i, :], AX.X, ALU.max, apply_absolute_value=True)
            link(last)
            dve.wait_ge(amaxed.h, NT)
            v.tensor_reduce(amax[:, 0:1], xmax[:, :], AX.X, ALU.max).then_inc(amaxed.h, 1)
            link(v.memset(att[:, 0, :], 1.0))
            for k in range(KT):
                last = v.tensor_scalar(bv_rep[:, k, :], bv_rep[:, k, :], b_t[:, 2, k:k + 1], None, ALU.mult)
            last.then_inc(bvrep.h, 1)
            dve.wait_ge(gmaxed.h, 1)
            link(v.tensor_scalar(expo[:, :], gmax[:, 1:5].bitcast(I32), 23, None, ALU.logical_shift_right))
            link(v.tensor_scalar(expo[:, :], expo[:, :], -1.0, 268.0, ALU.mult, ALU.add))
            link(v.tensor_scalar(expo[:, :], expo[:, :], 167.0, None, ALU.min))
            link(v.tensor_scalar(sw[:, :].bitcast(I32), expo[:, :], 23, None, ALU.logical_shift_left))
            v.tensor_scalar(c4[:, 1:4], gmax[:, 1:4], float(D), None, ALU.mult)
            v.tensor_copy(d4[:, 1:3], gmax[:, 5:7])
            v.reciprocal(rw[:, :], sw[:, :]).then_inc(dconst.h, 1)
            dve.wait_ge(dconst.h, 1)
            dve.sem_inc(masked_n.h, 4)
            dve.sem_inc(ot_l.h, ot_l.credit)
            dve.sem_inc(y_sb.h, y_sb.credit)
            dve.sem_inc(pv.h, pv.credit)
            dve.sem_inc(o_sb.h, o_sb.credit)

            def scales(b):
                links = [0]

                def linkb(ins):
                    links[0] += 1
                    ins.then_inc(dlb.h, 1)
                    dve.wait_ge(dlb.h, dlb.at(b, 1 + links[0]))

                dve.wait_ge(gmaxed.h, gmaxed.at(b, 1))
                linkb(v.scalar_tensor_tensor(bound[:, :], c4[:, :], gmax[:, 0:1], d4[:, :], ALU.mult, ALU.add))
                linkb(v.tensor_scalar(expo[:, :], bound[:, :].bitcast(I32), 23, None, ALU.logical_shift_right))
                linkb(v.tensor_tensor(expo[:, :], target4[:, :], expo[:, :], ALU.subtract))
                linkb(v.tensor_tensor(expo[:, :], expo[:, :], cap4[:, :], ALU.min))
                linkb(v.tensor_scalar(sc[:, :].bitcast(I32), expo[:, :], 23, None, ALU.logical_shift_left))
                v.tensor_scalar(beta_t[:, 0, :], b_t[:, 0, :], sc[:, 1:2], None, ALU.mult)
                v.tensor_scalar(beta_t[:, 1, :], b_t[:, 1, :], sc[:, 2:3], None, ALU.mult)
                linkb(v.reciprocal(rx[:, :], sc[:, 0:1]))
                v.scalar_tensor_tensor(alpha[:, :], sc[:, 1:4], rx[:, :], rw[:, 0:3], ALU.mult, ALU.mult)\
                    .then_inc(scaled.h, 1)

            def mask_rows(b, t):
                for f in range(2):
                    i = 2 * t + f
                    dve.wait_ge(a_in[i % 4].h, a_in[i % 4].at(b, 16 * (i // 4 + 1)))
                    v.tensor_scalar(mask_n[:, t, f * HALF:(f + 1) * HALF], ar_ring[i % 4], 0.0, MASKED,
                                    ALU.is_equal, ALU.mult).then_inc(masked_n.h, 1)

            def x_lo(b, t):
                dve.wait_ge(xt_h.h, xt_h.at(b, t + 1))
                v.scalar_tensor_tensor(xt_lo[:, :, t * P:(t + 1) * P],
                                       gp[:, :].rearrange("p (k n) -> p k n", n=P), sc[:, 0:1],
                                       xt_hi[:, :, t * P:(t + 1) * P], ALU.mult, ALU.subtract)\
                    .then_inc(xt_l.h, 1)

            def mask_out(b, t):
                dve.wait_ge(mt_ps.h, mt_ps.at(b, t + 1))
                v.tensor_scalar(mask_t[:, :, t * P:(t + 1) * P], mt_bank(t), 1.0 / MASKED, None, ALU.mult)\
                    .then_inc(mt_sb[1].h, 1)

            scales(-1)
            for t in range(NT):
                x_lo(-1, t)
                mask_rows(-1, t)
                if t % 2:
                    i = t // 2
                    dve.wait_ge(whi.h, i + 1)
                    v.scalar_tensor_tensor(w_lo[:, i, :, :].rearrange("p k n -> p (k n)"), w32[i], sw[:, i:i + 1],
                                           w_hi[:, i, :, :].rearrange("p k n -> p (k n)"), ALU.mult, ALU.subtract)\
                        .then_inc(wlo.h, 1)
            for t in range(1, NT, 2):
                mask_out(-1, t)
            dve.wait_ge(bvwo.h, 1)
            dve.wait_ge(rows_in.h, 3 * 16)
            v.tensor_tensor(bo_b[:, :], op[:, :], bo_b[:, :], ALU.add).then_inc(bo_ready.h, 1)
            dve.wait_ge(zeroed.h, 3 + 8)
            for i in range(4):
                a = HD * (1 - i % 2)
                last = v.memset(k2[i][a:a + 3, :], SHIFT_UNIT)
            last.then_inc(fixed.h, 1)

            with dve.Fori(0, B) as b:
                def v_lo(t):
                    dve.wait_ge(v_h.h, v_h.at(b, t + 1))
                    v.scalar_tensor_tensor(vt[:, t, :, 0:HD], og_bank[t % 2].rearrange("p (h d) -> p h d", d=HD),
                                           alpha[:, 2:3], vt[:, t, :, HD:2 * HD], ALU.mult, ALU.subtract)\
                        .then_inc(v_l.h, 1)

                def x_max(t):
                    dve.wait_ge(x_in[t % XR].h, x_in[t % XR].at(b, 16 * (t // XR + 1)))
                    v.tensor_reduce(xmax[:, t:t + 1], xr[:, t % XR, :], AX.X, ALU.max,
                                    apply_absolute_value=True).then_inc(xmaxed.h, 1)

                def maxima(h, t):
                    dve.wait_ge(mx_ps.h, mx_ps.at(b, 8 * h + t + 1))
                    dve.sem_inc(dve_wait.h, 1)
                    s2 = mx[:, :, :].rearrange("p a n -> p (a n)")
                    v.tensor_tensor_reduce(out=s2, in0=s2, in1=mask_n[:, t, :], scale=-1.0 / SHIFT_UNIT,
                                           scalar=3.0e38, op0=ALU.add, op1=ALU.min,
                                           accum_out=gam[:, t:t + 1]).then_inc(mx_done.h, 1)

                def shift_lo(h, f):
                    dve.wait_ge(gam_h.h, gam_h.at(b, 2 * h + f + 1))
                    v.tensor_tensor(shl[:, 4 * f:4 * f + 4, 1], gam[:, 4 * f:4 * f + 4],
                                    shl[:, 4 * f:4 * f + 4, 0], ALU.subtract).then_inc(gam_l.h, 1)

                def normalise(u):
                    h, f = u // 2, u % 2
                    dve.wait_ge(pv.h, pv.at(b, 2 * u + 2))
                    dve.wait_ge(o_sb.h, o_sb.at(b, u))
                    o = op[:, 0:4 * OW].rearrange("p (t w) -> p t w", w=OW)
                    v.reciprocal(rinv[:, :], o[:, :, HD]).then_inc(o_inv.h, 1)
                    dve.wait_ge(o_inv.h, o_inv.at(b, u + 1))
                    v.tensor_tensor(att[:, 4 * f:4 * f + 4, h * HD:(h + 1) * HD], o[:, :, 0:HD],
                                    rinv[:, :].unsqueeze(2).to_broadcast([P, 4, HD]), ALU.mult)\
                        .then_inc(o_sb.h, 1)

                dve.wait_ge(scaled.h, scaled.at(b, 0))
                dve.wait_ge(ex_sb.h, ex_sb.at(b, 0))
                v.tensor_scalar(so[:, :], sc[:, 3:4], sw[:, 3:4], None, ALU.mult)
                v.tensor_scalar(sqk[:, :], sc[:, 1:2], sc[:, 2:3], float(HD) ** 0.5, ALU.mult, ALU.mult)\
                    .then_inc(dlb.h, 1)
                dve.wait_ge(dlb.h, dlb.at(b, 1))
                v.reciprocal(gsc[:, :], sqk[:, :])
                v.reciprocal(ao[:, :], so[:, :])
                v.tensor_scalar(shl[:, :, 2], ones8[:, :], sqk[:, :], LN64 / SHIFT_UNIT,
                                ALU.mult, ALU.mult).then_inc(rescaled.h, 1)
                for t in range(NT):
                    if t < NT - 1:
                        v_lo(t)
                    maxima(0, t)
                    if t == NT - 1:
                        v_lo(t)
                    if t < NT - 1:
                        x_max(t)
                    if t == 3:
                        shift_lo(0, 0)
                for h, s in STEPS:
                    c, u = 8 * h + s, 2 * h + s // 4
                    if s % 4 == 0 and u >= 2:
                        normalise(u - 2)
                    dve.wait_ge(st_ps.h, st_ps.at(b, c + 1))
                    f, i = s // 4, s % 4
                    chunk = st[c % 2][:, :, :]
                    v.scalar_tensor_tensor(chunk, mask_t[:, 2 * i:2 * i + 2, f * HALF:(f + 1) * HALF], MASKED,
                                           chunk, ALU.mult, ALU.add).then_inc(st_mk.h, 1)
                    if h < H - 1:
                        maxima(h + 1, s)
                    if h == X_HEAD:
                        x_lo(b, s)
                    if s == 0:
                        shift_lo(h, 1)
                    if c == 2:
                        x_max(NT - 1)
                    if s == 4 and h < H - 1:
                        shift_lo(h + 1, 0)
                    if (h, s) == (4, 0):
                        dve.wait_ge(xmaxed.h, xmaxed.at(b, NT))
                        v.tensor_reduce(amax[:, 0:1], xmax[:, :], AX.X, ALU.max).then_inc(xm_all.h, 1)
                    if (h, s) == (4, 5):
                        dve.wait_ge(grp32.h, grp32.at(b, 12))
                        scales(b)
                    if h == H - 1:
                        if s == 6:
                            mask_out(b, 1)
                        mask_rows(b, s)
                normalise(2 * H - 2)
                def att_lo(t):
                    dve.wait_ge(ot_h.h, ot_h.at(b, t + 1))
                    v.tensor_tensor(ot_lo[t % 4], mx[:, t % 2, :].rearrange("p (k n) -> p k n", n=P),
                                    ot_hi[t % 4], ALU.subtract).then_inc(ot_l.h, 1)

                mask_out(b, 3)
                mask_out(b, 5)
                att_lo(0)
                att_lo(1)
                mask_out(b, 7)
                normalise(2 * H - 1)
                for t in range(NT + 1):
                    if t < NT:
                        dve.wait_ge(z_ps.h, z_ps.at(b, t + 1))
                        dve.wait_ge(xb.h, xb.at(b, t + 1))
                        dve.wait_ge(y_out[t % 4].h, y_out[t % 4].at(b, 16 * (t // 4)))
                        v.scalar_tensor_tensor(yr[:, t % 4, :], st_bank[t % 4], ao[:, :],
                                               xr[:, (2 * NT + t) % XR, :], ALU.mult, ALU.add).then_inc(y_sb.h, 1)
                    if t + 2 < NT:
                        att_lo(t + 2)
                    if t < NT:
                        dve.wait_ge(y_sb.h, y_sb.at(b, t + 1))
                        v.bn_stats(stats[:, t % 2, :], yr[:, t % 4, :]).then_inc(y_st.h, 1)
                    if t >= 1:
                        z = t - 1
                        dve.wait_ge(y_mv.h, y_mv.at(b, z + 1))
                        v.scalar_tensor_tensor(yr[:, z % 4, :], yr[:, z % 4, :], mv[:, z % 2, 0:1], gamma_b[:, :],
                                               ALU.subtract, ALU.mult).then_inc(y_ga.h, 1)
                    if t < NT:
                        dve.wait_ge(y_st.h, y_st.at(b, t + 1))
                        dve.sem_inc(dve_wait.h, 1)
                        v.bn_aggr(mv[:, t % 2, :], stats[:, t % 2, :]).then_inc(y_mv.h, 1)
                    if t >= 1:
                        z = t - 1
                        dve.wait_ge(y_ga.h, y_ga.at(b, z + 1))
                        dve.wait_ge(y_rs.h, y_rs.at(b, z + 1))
                        v.scalar_tensor_tensor(yr[:, z % 4, :], yr[:, z % 4, :], rstd[:, z % 2:z % 2 + 1],
                                               beta_b[:, :], ALU.mult, ALU.add).then_inc(y_be.h, 1)

        @block.gpsimd
        def _(pool):
            g = nc.gpsimd
            for m in (id32, id16, idbf):
                g.memset(m[:, :], 0.0).then_inc(zeroed.h, 1)
            pool.wait_ge(zeroed.h, 3)
            for m in (id32, id16, idbf):
                g.affine_select(out=m[:, :], in_=m[:, :], compare_op=ALU.not_equal, fill=1.0, base=0,
                                pattern=[[-1, P]], channel_multiplier=1).then_inc(consts.h, 1)
            for i in range(4):
                g.memset(k2[i][:, :], 0.0).then_inc(zeroed.h, 1)
                g.memset(q2[i][:, :], 0.0).then_inc(zeroed.h, 1)
            pool.wait_ge(amaxed.h, NT + 1)
            g.partition_all_reduce(gmax[:, :], amax[:, :], P, ABSMAX).then_inc(gmaxed.h, 1)
            pool.sem_inc(grp_l.h, 2)
            pool.sem_inc(p_l.h, p_l.credit)

            def group_lo(b, gr):
                w, f = GROUPS[gr % 4]
                pool.wait_ge(grp_h.h, grp_h.at(b, gr + 1))
                part = stage[:, 1 - w, :, f * HALF:(f + 1) * HALF]
                g.tensor_tensor(part[:, 1, :], proj[:, gr % 2, :], part[:, 0, :], ALU.subtract)\
                    .then_inc(grp_l.h, 1)

            for gr in range(12, 16):
                group_lo(-1, gr)

            with pool.Fori(0, B) as b:
                for gr in range(2):
                    group_lo(b, gr)
                for h, s in STEPS:
                    c, u = 8 * h + s, 2 * h + s // 4
                    pool.wait_ge(p_h.h, p_h.at(b, c + 1))
                    m = slice(2 * (s % 4), 2 * (s % 4) + 2)
                    g.tensor_tensor(pr_lo[u % 2][:, m, :].rearrange("p a n -> p (a n)"), ex[:, c % 2, :],
                                    pr_hi[u % 2][:, m, :].rearrange("p a n -> p (a n)"), ALU.subtract)\
                        .then_inc(p_l.h, 1)
                    if c in TO_LO:
                        group_lo(b, TO_LO[c])
                    if (h, s) == (4, 2):
                        pool.wait_ge(xm_all.h, xm_all.at(b, 1))
                        pool.wait_ge(scaled.h, scaled.at(b, 0))
                        pool.sem_inc(pool_wait.h, 1)
                        g.partition_all_reduce(gmax[:, 0:1], amax[:, 0:1], P, ABSMAX).then_inc(gmaxed.h, 1)
                group_lo(b, 14)
                group_lo(b, 15)
                for t in range(NT + 1):
                    if t < NT:
                        n = 2 * NT + t
                        pool.wait_ge(x_in[n % XR].h, x_in[n % XR].at(b, 16 * (n // XR + 1)))
                        g.tensor_tensor(xr[:, n % XR, :], xr[:, n % XR, :], bo_b[:, :], ALU.add).then_inc(xb.h, 1)
                    if t >= 1:
                        z = t - 1
                        pool.wait_ge(y_mv.h, y_mv.at(b, z + 1))
                        g.tensor_tensor(vpe[:, z % 2:z % 2 + 1], mv[:, z % 2, 1:2], eps[:, :], ALU.add)\
                            .then_inc(y_ve.h, 1)
                        pool.wait_ge(y_ve.h, y_ve.at(b, z + 1))
                        g.tensor_tensor(rstd[:, z % 2:z % 2 + 1], vpe[:, z % 2:z % 2 + 1], mhalf[:, :], ALU.pow)\
                            .then_inc(y_rs.h, 1)


_INS = ['x', 'adj', 'L0_gnn_Wq', 'L0_gnn_bq', 'L0_gnn_Wk', 'L0_gnn_bk', 'L0_gnn_Wv', 'L0_gnn_bv',
        'L0_gnn_Wo', 'L0_gnn_bo', 'L0_gnn_gamma', 'L0_gnn_beta']


def kernel(**inputs):
    import numpy as np
    import concourse.bacc as bacc
    from concourse.bass_utils import run_bass_kernel_spmd

    nc = bacc.Bacc("TRN2", target_bir_lowering=False, num_devices=1)
    arrays, args = {}, []
    for name in _INS:
        a = np.ascontiguousarray(inputs[name])
        arrays[f"in_{name}"] = a
        args.append(nc.dram_tensor(f"in_{name}", a.shape, mybir.dt.from_np(a.dtype), kind="ExternalInput").ap())
    out = nc.dram_tensor("result", inputs["x"].shape, F32, kind="ExternalOutput").ap()
    gnn_attention(nc, *args, out)
    r = run_bass_kernel_spmd(nc, [arrays], core_ids=[0])
    return r.results[0]["result"]
```
